# Optimizing a Trainium2 kernel written in Bass

```python
import numpy as np
import jax
import jax.numpy as jnp

def _softmax(x, axis=-1):
    return jax.nn.softmax(x, axis=axis)

def _gelu(x):
    return jax.nn.gelu(x, approximate=True)

def _silu(x):
    return jax.nn.silu(x)

def _sigmoid(x):
    return jax.nn.sigmoid(x)

def _layernorm(x, axis=-1, eps=1e-05):
    m = jnp.mean(x, axis=axis, keepdims=True)
    v = jnp.var(x, axis=axis, keepdims=True)
    return (x - m) / jnp.sqrt(v + eps)

def _scatter_add(tgt, idx, src, axis=0):
    return tgt.at[idx].add(src)

def _segment_sum(src, seg, n):
    return jax.ops.segment_sum(src, seg, n)
kernel_name = 'mk_flamingo_gated_d1_seqx_r8_dca19f'

def setup_inputs(seed: int=0):
    np.random.seed(seed)
    _w = jnp.asarray

    def _rec_inputs():
        import jax
        import jax.numpy as jnp
        _rk = jax.random.key(seed)
        x = -0.0002928 + 1 * jax.random.normal(jax.random.fold_in(_rk, 1), (32, 128, 128), jnp.float32)
        _lenS = 128 - jax.random.randint(jax.random.fold_in(_rk, 7), (32,), 0, max(1, 128 // 4) + 1, jnp.int32)
        _lenS2 = 128 - jax.random.randint(jax.random.fold_in(_rk, 8), (32,), 0, max(1, 128 // 4) + 1, jnp.int32)
        _ctx_1024P = jax.random.normal(jax.random.fold_in(_rk, 11), (32, 16, 128), jnp.float32)
        _ctx_1024c = jax.random.dirichlet(jax.random.fold_in(_rk, 511), 0.3 * jnp.ones((16,), jnp.float32), (32, 128))
        _ctx_1024t = jnp.einsum('bsk,bkd->bsd', _ctx_1024c, _ctx_1024P)
        _ctx_1024t = _ctx_1024t * jax.lax.rsqrt(jnp.mean(jnp.square(_ctx_1024t)) + 1e-12) * 0.953939
        ctx_1024 = -1.39393e-06 + 0.999914 * (_ctx_1024t + 0.3 * jax.random.normal(jax.random.fold_in(_rk, 611), (32, 128, 128), jnp.float32))
        _g = jax.random.normal(jax.random.fold_in(_rk, 9001), (2, 1), jnp.float32)
        _g = jnp.sign(_g) * jnp.maximum(jnp.abs(_g), 1.0) + (_g == 0) * 1.0
        g_xattn = _g[0]
        g_ffn = _g[1]
        return (x, ctx_1024, g_xattn, g_ffn)
    x, ctx_1024, g_xattn, g_ffn = _rec_inputs()

    def _L0_xattn_setup():
        import jax, jax.numpy as jnp
        import numpy as np
        import math
        N_HEAD = 16
        key = jax.random.key(seed)
        ks = jax.random.split(key, 11)
        B, T, D = (2, 256, 128)
        s = 0.02
        return {'q': jax.random.normal(ks[0], (B, T, D), jnp.float32), 'k': jax.random.normal(ks[1], (B, T, D), jnp.float32), 'v': jax.random.normal(ks[2], (B, T, D), jnp.float32), 'Wq': jax.random.normal(ks[3], (D, D), jnp.float32) * s, 'bq': jax.random.normal(ks[4], (D,), jnp.float32) * s, 'Wk': jax.random.normal(ks[5], (D, D), jnp.float32) * s, 'bk': jax.random.normal(ks[6], (D,), jnp.float32) * s, 'Wv': jax.random.normal(ks[7], (D, D), jnp.float32) * s, 'bv': jax.random.normal(ks[8], (D,), jnp.float32) * s, 'Wc': jax.random.normal(ks[9], (D, D), jnp.float32) * s, 'bc': jax.random.normal(ks[10], (D,), jnp.float32) * s}
    _L0_xattn_all = _L0_xattn_setup()
    _L0_xattn_in = {k: v for k, v in _L0_xattn_all.items() if k in ('Wq', 'bq', 'Wk', 'bk', 'Wv', 'bv', 'Wc', 'bc')}
    del _L0_xattn_all

    def _L0_ffn_setup():
        import jax, jax.numpy as jnp
        import numpy as np
        import math
        BETA = 0.9
        THRESHOLD = 1.0
        NUM_STEPS = 5
        ALPHA = 2.0

        @jax.custom_vjp
        def spike_fn(u):
            return (u > 0).astype(u.dtype)

        def _spike_fwd(u):
            return (spike_fn(u), u)

        def _spike_bwd(u, g):
            s = jnp.pi / 2.0 * ALPHA * u
            return (g * (ALPHA / 2.0) / (1.0 + s * s),)
        spike_fn.defvjp(_spike_fwd, _spike_bwd)
        key = jax.random.key(seed)
        k1, k2, k3 = jax.random.split(key, 3)
        n_embd = 128
        x = jax.random.normal(k1, (4, 256, n_embd), dtype=jnp.float32)
        W_fc = jax.random.normal(k2, (4 * n_embd, n_embd), dtype=jnp.float32) / math.sqrt(n_embd)
        W_proj = jax.random.normal(k3, (n_embd, 4 * n_embd), dtype=jnp.float32) / math.sqrt(4 * n_embd)
        return {'x': x, 'W_fc': W_fc, 'W_proj': W_proj}
    _L0_ffn_all = _L0_ffn_setup()
    _L0_ffn_in = {k: v for k, v in _L0_ffn_all.items() if k in ('W_fc', 'W_proj')}
    del _L0_ffn_all
    return {'x': x, 'ctx_1024': ctx_1024, 'g_xattn': g_xattn, 'g_ffn': g_ffn, 'L0_xattn_Wq': _L0_xattn_in['Wq'], 'L0_xattn_bq': _L0_xattn_in['bq'], 'L0_xattn_Wk': _L0_xattn_in['Wk'], 'L0_xattn_bk': _L0_xattn_in['bk'], 'L0_xattn_Wv': _L0_xattn_in['Wv'], 'L0_xattn_bv': _L0_xattn_in['bv'], 'L0_xattn_Wc': _L0_xattn_in['Wc'], 'L0_xattn_bc': _L0_xattn_in['bc'], 'L0_ffn_W_fc': _L0_ffn_in['W_fc'], 'L0_ffn_W_proj': _L0_ffn_in['W_proj']}

def reference(x, ctx_1024, g_xattn, g_ffn, L0_xattn_Wq, L0_xattn_bq, L0_xattn_Wk, L0_xattn_bk, L0_xattn_Wv, L0_xattn_bv, L0_xattn_Wc, L0_xattn_bc, L0_ffn_W_fc, L0_ffn_W_proj):
    import jax
    import jax.numpy as jnp

    def _L0_xattn_ref(q, k, v, Wq, bq, Wk, bk, Wv, bv, Wc, bc):
        import jax, jax.numpy as jnp
        import numpy as np
        import math
        N_HEAD = 16
        B, T, D = q.shape
        H = N_HEAD
        nd = D // H

        def proj(x, W, b):
            y = x @ W.T + b
            return y.reshape(B, T, H, nd).transpose(0, 2, 1, 3)
        qh = proj(q, Wq, bq)
        kh = proj(k, Wk, bk)
        vh = proj(v, Wv, bv)
        z = jnp.einsum('bhqd,bhkd->bhqk', qh, kh) / math.sqrt(nd)
        mask = jnp.tril(jnp.ones((T, T), dtype=bool))
        z = jnp.where(mask, z, -jnp.inf)
        attn = jax.nn.softmax(z, axis=-2)
        out = jnp.einsum('bhqk,bhkd->bhqd', attn, vh)
        out = out.transpose(0, 2, 1, 3).reshape(B, T, D)
        return out @ Wc.T + bc

    def _L0_ffn_ref(x, W_fc, W_proj):
        import jax, jax.numpy as jnp
        import numpy as np
        import math
        BETA = 0.9
        THRESHOLD = 1.0
        NUM_STEPS = 5
        ALPHA = 2.0

        @jax.custom_vjp
        def spike_fn(u):
            return (u > 0).astype(u.dtype)

        def _spike_fwd(u):
            return (spike_fn(u), u)

        def _spike_bwd(u, g):
            s = jnp.pi / 2.0 * ALPHA * u
            return (g * (ALPHA / 2.0) / (1.0 + s * s),)
        spike_fn.defvjp(_spike_fwd, _spike_bwd)
        h = jnp.square(jax.nn.relu(jnp.einsum('bsd,fd->bsf', x, W_fc)))
        y = jnp.einsum('bsf,df->bsd', h, W_proj)

        def step(mem, _):
            reset = jax.lax.stop_gradient(spike_fn(mem - THRESHOLD))
            mem_new = BETA * mem + y - reset * THRESHOLD
            spk = spike_fn(mem_new - THRESHOLD)
            return (mem_new, spk)
        mem0 = jnp.zeros_like(y)
        _, spks = jax.lax.scan(step, mem0, None, length=NUM_STEPS)
        return jnp.sum(spks, axis=0) / NUM_STEPS
    x = x + jnp.tanh(g_xattn[0]) * _L0_xattn_ref(_layernorm(x, axis=-1), ctx_1024, ctx_1024, L0_xattn_Wq, L0_xattn_bq, L0_xattn_Wk, L0_xattn_bk, L0_xattn_Wv, L0_xattn_bv, L0_xattn_Wc, L0_xattn_bc)
    x = x + jnp.tanh(g_ffn[0]) * _L0_ffn_ref(_layernorm(x, axis=-1), L0_ffn_W_fc, L0_ffn_W_proj)
    return x

_drawn_inputs = setup_inputs


def setup_inputs(seed=0):
    import zlib

    import numpy as np

    out = dict(_drawn_inputs(seed))
    spreads = {}
    factors = {'L0_xattn_Wq': 8.0,
     'L0_xattn_bq': 64.0,
     'L0_xattn_Wk': 8.0,
     'L0_xattn_bk': 26.482,
     'L0_xattn_bv': 4.925}
    for name, (base, spread) in spreads.items():
        noise = np.random.default_rng([zlib.crc32(name.encode()), seed]).standard_normal(out[name].shape)
        drawn = base * np.exp(spread * noise) if base else spread * noise
        out[name] = jnp.asarray(drawn.astype(out[name].dtype))
    for name, factor in factors.items():
        out[name] = (out[name] * factor).astype(out[name].dtype)
    return out
```

```python
from contextlib import ExitStack

import concourse.bass as bass
from concourse import mybir

ALU = mybir.AluOpType
ACT = mybir.ActivationFunctionType
AX_X = mybir.AxisListType.X
F32 = mybir.dt.float32
BF16 = mybir.dt.bfloat16

B = 32
T = 128
D = 128
H = 16
ND = D // H
FF = 4 * D
EPS = 1e-5
SCALE = float(ND) ** -0.5
MASKED = -1e30
BETA = 0.9
THRESHOLD = 1.0
STEPS = 5

PG = 4
NPG = B // PG
G = 2
NG = B // G
U = 4
J = H // U
PARTS = 3
PAIRS = [(i, j) for i in range(PARTS) for j in range(PARTS)]
ROWS = 96
STACK_INC = 16 * 2 * len(PAIRS)
SPIKE_OPS = 2 + 3 * (STEPS - 1)
VP = T + ND
assert len(PAIRS) * ND <= ROWS


def gated_block_kernel(nc, x, ctxT, g_xattn, g_ffn, WqT, bq, WkT, bk, WvT, bv, WcT, bc, WfcT, WprojT, out):
    with ExitStack() as ctx:
        def sb(name, shape, dt=F32):
            return ctx.enter_context(nc.sbuf_tensor(name, shape, dt))

        def pb(name):
            return ctx.enter_context(nc.psum_tensor(name, [128, 512], F32))

        def sem(name):
            return ctx.enter_context(nc.semaphore(name))

        wq = sb("wq", [D, D])
        wk = sb("wk", [D, D])
        wv = sb("wv", [D, D])
        wc = sb("wc", [D, D])
        wfc = sb("wfc", [D, FF])
        wproj = sb("wproj", [128, FF // 128, D])
        bq_col = sb("bq_col", [D, 1])
        bq_scaled = sb("bq_scaled", [D, 1])
        bk_col = sb("bk_col", [D, 1])
        bv_row = sb("bv_row", [128, D])
        bc_row = sb("bc_row", [128, D])
        gates = sb("gates", [128, 2])
        tanh_gates = sb("tanh_gates", [128, 2])
        spike_gain = sb("spike_gain", [128, 1])
        ident = sb("ident", [128, 128])
        ident_bf = sb("ident_bf", [128, 128], BF16)
        mask = sb("mask", [T, J * T], BF16)
        minus_half = sb("minus_half", [128, PG])
        eps = sb("eps", [128, PG])
        idle = sb("idle", [128, 1])

        x_all = sb("x_all", [T, B, D])
        v_all = sb("v_all", [T, B, D])

        ctx_t = sb("ctx_t", [D, 2, PG * T])
        stats1 = sb("stats1", [T, PG, 6])
        moments1 = sb("moments1", [T, PG, 2])
        var_eps1 = sb("var_eps1", [T, PG])
        rstd1 = sb("rstd1", [T, PG])
        xn1 = sb("xn1", [T, PG, D])
        xn1_t = sb("xn1_t", [D, PG * T])
        q_parts = sb("q_parts", [D, 2, PARTS, PG * T], BF16)
        k_parts = sb("k_parts", [D, 2, PARTS, PG * T], BF16)
        q_full = sb("q_full", [D, 2, PG * T])
        k_full = sb("k_full", [D, 2, PG * T])
        q_rest = sb("q_rest", [D, PG * T])
        k_rest = sb("k_rest", [D, PG * T])

        q_stack = [sb(f"q_stack{i}", [ROWS, H, G * T], BF16) for i in range(2)]
        k_stack = [sb(f"k_stack{i}", [ROWS, H, G * T], BF16) for i in range(2)]
        probs = [sb(f"probs{i}", [T, H, T]) for i in range(2)]
        neg_max = sb("neg_max", [T, 2, H])
        row_sum = sb("row_sum", [T, 2, H])
        inv_sum = sb("inv_sum", [T, H])
        v_pad = [sb(f"v_pad{i}", [T, U * VP]) for i in range(2)]
        attn_t = sb("attn_t", [D, T])
        stats2 = sb("stats2", [T, 6])
        moments2 = sb("moments2", [T, 2])
        var_eps2 = sb("var_eps2", [T, 1])
        rstd2 = sb("rstd2", [T, 1])
        xn2 = sb("xn2", [T, 2, D])
        xn2_t = sb("xn2_t", [D, G * T])
        relu = sb("relu", [128, 2, 2 * G * T])
        hidden = sb("hidden", [128, 2, 2 * G * T])
        y_t = sb("y_t", [D, G * T])
        mem = sb("mem", [D, G * T])
        charge = sb("charge", [D, G * T])
        count = sb("count", [D, G * T], BF16)

        q_dram = nc.dram_tensor("q_dram", [PARTS, D, B * T], BF16).ap()
        k_dram = nc.dram_tensor("k_dram", [PARTS, D, B * T], BF16).ap()

        bank = [pb(f"bank{i}") for i in range(8)]
        k_ps, q_ps, v_ps, t_ps = bank[0:2], bank[2:4], bank[4:6], bank[6:8]
        s_ps = bank[0:4]
        o_ps = bank[4][:, 0:T]
        y_ps = bank[4][:, 128:128 + D]
        tr_ps = bank[5]
        f_ps = bank[6:8]
        count_ps = tr_ps[:, 256:256 + G * D // 2].bitcast(BF16)

        consts_loaded = sem("consts_loaded")
        x_loaded = [sem(f"x_loaded{i}") for i in range(2)]
        ctx_loaded = [sem(f"ctx_loaded{i}") for i in range(2)]
        zeroed = sem("zeroed")
        tables_ready = sem("tables_ready")
        filled = sem("filled")
        gates_ready = sem("gates_ready")
        gates_scaled = sem("gates_scaled")
        bq_ready = sem("bq_ready")
        stats1_done = sem("stats1_done")
        moments1_ready = sem("moments1_ready")
        var_eps1_ready = sem("var_eps1_ready")
        rstd1_ready = sem("rstd1_ready")
        xn1_ready = sem("xn1_ready")
        xn1_turned = sem("xn1_turned")
        xn1_t_ready = sem("xn1_t_ready")
        k_projected = sem("k_projected")
        q_projected = sem("q_projected")
        v_projected = sem("v_projected")
        k_full_ready = sem("k_full_ready")
        q_full_ready = sem("q_full_ready")
        v_ready = sem("v_ready")
        q_rest_ready = sem("q_rest_ready")
        q_mid_ready = sem("q_mid_ready")
        q_split = sem("q_split")
        k_rest_ready = sem("k_rest_ready")
        k_split = sem("k_split")
        parts_stored = [sem(f"parts_stored{i}") for i in range(2)]
        stack_loaded = [sem(f"stack_loaded{i}") for i in range(2)]
        scores_ready = sem("scores_ready")
        max_ready = sem("max_ready")
        exp_done = sem("exp_done")
        inv_ready = sem("inv_ready")
        v_pad_ready = sem("v_pad_ready")
        pv_done = sem("pv_done")
        attn_t_ready = sem("attn_t_ready")
        y_ready = sem("y_ready")
        bias_added = sem("bias_added")
        x2_ready = sem("x2_ready")
        stats2_done = sem("stats2_done")
        moments2_ready = sem("moments2_ready")
        var_eps2_ready = sem("var_eps2_ready")
        rstd2_ready = sem("rstd2_ready")
        xn2_ready = sem("xn2_ready")
        xn2_turned = sem("xn2_turned")
        xn2_t_ready = sem("xn2_t_ready")
        fc_done = sem("fc_done")
        relu_ready = sem("relu_ready")
        hidden_ready = sem("hidden_ready")
        proj_done = sem("proj_done")
        spike_op_done = sem("spike_op_done")
        count_turned = sem("count_turned")
        result_ready = sem("result_ready")
        stored = sem("stored")

        x_tok = x.rearrange("b t d -> t b d")
        out_tok = out.rearrange("b t d -> t b d")
        N_CONSTS = 14

        def stage1(eng, body):
            body(0, 0)
            body(1, 1)
            with eng.Fori(0, (NPG - 4) // 2) as t:
                body(t * 2 + 2, 2)
                body(t * 2 + 3, 3)
            body(NPG - 2, NPG - 2)
            body(NPG - 1, NPG - 1)

        def stage2(eng, body):
            first, last = 8, B + 6
            for s in range(first):
                body(s, s)
            with eng.Fori(0, (B - first) // 4) as t:
                for i in range(4):
                    body(t * 4 + (first + i), first + i)
            for s in range(B, last):
                body(s, s)

        def loads_of(g, p):
            return 16 * (g // 2 + 1) if isinstance(g, int) else (g - p) * 8 + 16

        def stored_before(g, g0):
            return 32 * (g // 2) if isinstance(g, int) else (g - g0 % 2) * 16

        def live(s0):
            odd = s0 % 2 == 1
            return dict(
                scores=s0 < B,
                attend=1 <= s0 <= B,
                turn=2 <= s0 <= B + 1,
                fc=odd and 3 <= s0 <= B + 1,
                proj=not odd and 4 <= s0 <= B + 2,
                spikes_a=odd and 5 <= s0 <= B + 3,
                spikes_b=not odd and 6 <= s0 <= B + 4,
                finish=odd and 7 <= s0 <= B + 5,
            )

        def group_of(s, s0, lag):
            if isinstance(s, int):
                return (s - lag) // 2
            return ((s - s0) // 2) + (s0 - lag) // 2

        def settle(dve):
            dve.memset(idle[:], 0.0)

        block = ctx.enter_context(nc.Block())

        @block.sync
        def _(sp):
            def load(g, g0):
                p = g0 % 2
                if g0 >= 2:
                    sp.wait_ge(moments1_ready, g - 1)
                sp.dma_start(x_all[:, bass.ds(g * PG, PG), :], x_tok[:, bass.ds(g * PG, PG), :]).then_inc(x_loaded[p], 16)
                if g0 >= 2:
                    sp.wait_ge(k_projected, g - 1)
                    sp.wait_ge(v_projected, g - 1)
                sp.dma_start(ctx_t[:, p, :], ctxT[:, bass.ds(g * (PG * T), PG * T)]).then_inc(ctx_loaded[p], 16)

            def keep_parts(g, g0):
                p = g0 % 2
                for parts, dram, split in ((k_parts, k_dram, k_split), (q_parts, q_dram, q_split)):
                    sp.wait_ge(split, g + 1)
                    sp.dma_start(dram[:, :, bass.ds(g * (PG * T), PG * T)].rearrange("s r t -> r s t"),
                                 parts[:, p, :, :]).then_inc(parts_stored[p], 16)

            def stack(g, g0):
                p = g0 % 2
                if g0 >= 2:
                    sp.wait_ge(scores_ready, g * (G * U) - G * U)
                for c, (i, j) in enumerate(PAIRS):
                    rows = slice(c * ND, (c + 1) * ND)
                    for dst, dram, part in ((q_stack, q_dram, i), (k_stack, k_dram, j)):
                        src = dram[part, :, bass.ds(g * (G * T), G * T)].rearrange("(h d) t -> d h t", d=ND)
                        sp.dma_start(dst[p][rows, :, :], src).then_inc(stack_loaded[p], 16)

            load(0, 0)
            load(1, 1)

            def body(g, g0):
                if g0 < NPG - 2:
                    load(g + 2, g0 + 2)
                keep_parts(g, g0)

            stage1(sp, body)
            sp.wait_ge(zeroed, 2)
            for p in range(2):
                sp.wait_ge(parts_stored[p], 16 * NPG)
            for g in range(2):
                stack(g, g)

            def store(f):
                sp.dma_start(out_tok[:, bass.ds(f * G, G), :], x_all[:, bass.ds(f * G, G), :]).then_inc(stored, 16)

            for g in range(2, 4):
                stack(g, g)
            with sp.Fori(0, (NG - 4) // 2) as t:
                for i in range(2):
                    stack(t * 2 + (4 + i), 4 + i)
                    sp.wait_ge(result_ready, t * 2 + (i + 1))
                    store(t * 2 + i)
            for f in range(NG - 4, NG):
                sp.wait_ge(result_ready, f + 1)
                store(f)
            sp.wait_ge(stored, 16 * NG)

        @block.scalar
        def _(act):
            for dst, src in (
                (gates[:, 0:1], g_xattn.partition_broadcast(128)), (gates[:, 1:2], g_ffn.partition_broadcast(128)),
                (wk[:], WkT), (bk_col[:], bk), (wv[:], WvT), (wq[:], WqT), (bq_col[:], bq),
                (bv_row[:], bv.partition_broadcast(128)), (bc_row[:], bc.partition_broadcast(128)),
                (wc[:], WcT), (wfc[:], WfcT),
            ):
                act.dma_start(dst, src).then_inc(consts_loaded, 16)
            act.dma_start(wproj[:], WprojT.rearrange("(c f) d -> f c d", f=128)).then_inc(consts_loaded, 16)
            act.wait_ge(consts_loaded, 16 * 12)
            act.activation(tanh_gates[:], gates[:], ACT.Tanh).then_inc(gates_ready, 1)
            act.mul(bq_scaled[:], bq_col[:], SCALE).then_inc(bq_ready, 1)
            act.wait_ge(bq_ready, 1)

            def turn_evac(g):
                act.wait_ge(xn1_turned, g + 1)
                act.activation(xn1_t[:], t_ps[0][:], ACT.Copy).then_inc(xn1_t_ready, 1)

            turn_evac(0)

            def body(g, g0):
                p = g0 % 2
                act.wait_ge(k_projected, g + 1)
                if g0 >= 2:
                    act.wait_ge(k_split, g - 1)
                    act.wait_ge(parts_stored[p], stored_before(g, g0))
                act.activation(k_full[:, p, :], k_ps[p][:], ACT.Identity, bias=bk_col[:])
                act.activation(k_parts[:, p, 0, :], k_ps[p][:], ACT.Identity, bias=bk_col[:]).then_inc(k_full_ready, 1)
                act.wait_ge(q_projected, g + 1)
                if g0 >= 2:
                    act.wait_ge(q_split, g - 1)
                act.activation(q_full[:, p, :], q_ps[p][:], ACT.Identity, bias=bq_scaled[:], scale=SCALE)
                act.activation(q_parts[:, p, 0, :], q_ps[p][:], ACT.Identity, bias=bq_scaled[:], scale=SCALE).then_inc(q_full_ready, 1)
                if g0 < NPG - 1:
                    turn_evac(g + 1)

            stage1(act, body)

            def slot(s, s0):
                on = live(s0)
                p = s0 % 2

                def exps(u):
                    act.wait_ge(max_ready, s * U + (u + 1))
                    for j in range(J):
                        h = u * J + j
                        e = act.activation(probs[p][:, h, :], s_ps[u][:, j * T:(j + 1) * T], ACT.Exp,
                                           bias=neg_max[:, p, h:h + 1], accum_out=row_sum[:, p, h:h + 1])
                    e.then_inc(exp_done, 1)

                def relus(half):
                    f = group_of(s, s0, 3)
                    act.wait_ge(fc_done, f * 2 + (half + 1))
                    if s0 >= 5:
                        act.wait_ge(hidden_ready, f * 2 + (half - 1))
                    act.activation(relu[:, half, :], f_ps[half][:], ACT.Relu).then_inc(relu_ready, 1)

                if on["scores"]:
                    if s0 >= 2:
                        act.wait_ge(pv_done, s - 1)
                        act.wait_ge(inv_ready, s - 1)
                    exps(0)
                    exps(1)
                    exps(2)
                if on["fc"]:
                    relus(0)
                if on["scores"]:
                    exps(3)
                if on["fc"]:
                    relus(1)

            stage2(act, slot)

        @block.gpsimd
        def _(pool):
            pool.memset(ident[:], 0.0)
            pool.memset(ident_bf[:], 0.0)
            pool.memset(minus_half[:], -0.5)
            pool.memset(eps[:], EPS)
            pool.memset(mask[:], 0.0).then_inc(filled, 1)
            pool.wait_ge(filled, 1)
            for t in (ident, ident_bf):
                pool.affine_select(out=t[:], in_=t[:], compare_op=ALU.not_equal, fill=1.0, base=0,
                                   pattern=[[-1, 128]], channel_multiplier=1)
            mask_v = mask[:].rearrange("p (j q) -> p j q", j=J)
            pool.affine_select(out=mask_v, in_=mask_v, compare_op=ALU.is_ge, fill=MASKED, base=0,
                               pattern=[[0, J], [1, T]], channel_multiplier=-1).then_inc(tables_ready, 1)

            def rstd1_of(g, g0):
                if g0 >= 1:
                    pool.wait_ge(rstd1_ready, g)
                    pool.wait_ge(xn1_ready, g)
                pool.wait_ge(moments1_ready, g + 1)
                pool.tensor_tensor(var_eps1[:], moments1[:, :, 1], eps[:], ALU.add).then_inc(var_eps1_ready, 1)
                pool.wait_ge(var_eps1_ready, g + 1)
                pool.tensor_tensor(rstd1[:], var_eps1[:], minus_half[:], ALU.pow).then_inc(rstd1_ready, 1)

            for t in q_stack:
                pool.memset(t[:].rearrange("r h t -> r (h t)").bitcast(F32), 0.0)
            rstd1_of(0, 0)
            for t in v_pad:
                last = pool.memset(t[:], 0.0)
            last.then_inc(zeroed, 1)

            def body(g, g0):
                p = g0 % 2
                if g0 < NPG - 1:
                    rstd1_of(g + 1, g0 + 1)
                pool.wait_ge(k_full_ready, g + 1)
                if g0 >= 1:
                    pool.wait_ge(k_split, g)
                pool.tensor_tensor(k_rest[:], k_full[:, p, :], k_parts[:, p, 0, :], ALU.subtract)
                pool.tensor_tensor(k_parts[:, p, 1, :], k_full[:, p, :], k_parts[:, p, 0, :], ALU.subtract).then_inc(k_rest_ready, 1)
                pool.wait_ge(k_rest_ready, g + 1)
                pool.tensor_tensor(k_parts[:, p, 2, :], k_rest[:], k_parts[:, p, 1, :], ALU.subtract).then_inc(k_split, 1)

            stage1(pool, body)

            def slot(s, s0):
                on = live(s0)
                if on["scores"]:
                    if s0 == 0:
                        pool.wait_ge(gates_scaled, 2)
                        pool.wait_ge(xn1_ready, NPG)
                    xs = x_all[:, s, :] if isinstance(s, int) else x_all[:, bass.ds(s, 1), :].squeeze(1)
                    pool.tensor_tensor(xs, xs, bc_row[:], ALU.add).then_inc(bias_added, 1)
                if on["fc"]:
                    f = group_of(s, s0, 3)
                    for half in range(2):
                        pool.wait_ge(relu_ready, f * 2 + (half + 1))
                        if s0 >= 5 and half == 0:
                            pool.wait_ge(proj_done, f)
                        pool.tensor_tensor(hidden[:, half, :], relu[:, half, :], relu[:, half, :], ALU.mult)\
                            .then_inc(hidden_ready, 1)
                if on["attend"]:
                    if s0 >= 2:
                        pool.wait_ge(rstd2_ready, s - 1)
                        pool.wait_ge(xn2_ready, s - 1)
                    pool.wait_ge(moments2_ready, s)
                    pool.tensor_tensor(var_eps2[:], moments2[:, 1:2], eps[:, 0:1], ALU.add).then_inc(var_eps2_ready, 1)
                    pool.wait_ge(var_eps2_ready, s)
                    pool.tensor_tensor(rstd2[:], var_eps2[:], minus_half[:, 0:1], ALU.pow).then_inc(rstd2_ready, 1)

            stage2(pool, slot)

        @block.tensor
        def _(pe):
            pe.wait_ge(tables_ready, 1)
            pe.wait_ge(consts_loaded, 16 * 12)

            def turn(g):
                pe.wait_ge(xn1_ready, g + 1)
                for i in range(PG):
                    t = pe.transpose(t_ps[0][:, i * T:(i + 1) * T], xn1[:, i, :], ident[:])
                t.then_inc(xn1_turned, 1)

            turn(0)

            def body(g, g0):
                p = g0 % 2
                pe.wait_ge(ctx_loaded[p], loads_of(g, p))
                if g0 >= 2:
                    pe.wait_ge(k_full_ready, g - 1)
                pe.matmul(k_ps[p][:], wk[:], ctx_t[:, p, :], start=True, stop=True).then_inc(k_projected, 1)
                pe.wait_ge(xn1_t_ready, g + 1)
                if g0 >= 2:
                    pe.wait_ge(q_full_ready, g - 1)
                pe.matmul(q_ps[p][:], wq[:], xn1_t[:], start=True, stop=True).then_inc(q_projected, 1)
                if g0 >= 2:
                    pe.wait_ge(v_ready, g - 1)
                for i in range(PG):
                    m = pe.matmul(v_ps[p][:, i * D:(i + 1) * D], ctx_t[:, p, i * T:(i + 1) * T], wv[:], start=True, stop=True)
                m.then_inc(v_projected, 1)
                if g0 < NPG - 1:
                    turn(g + 1)

            stage1(pe, body)

            pe.wait_ge(zeroed, 2)
            pe.wait_ge(k_full_ready, NPG)
            pe.wait_ge(q_full_ready, NPG)
            pe.wait_ge(v_ready, NPG)

            def slot(s, s0):
                on = live(s0)
                p = s0 % 2
                buf, i = (s0 // G) % 2, s0 % G
                tok = slice(i * T, (i + 1) * T)

                def scores(u):
                    if u == 0 and i == 0:
                        pe.wait_ge(stack_loaded[buf], ((s - s0) // 4 + (s0 // 4 + 1)) * STACK_INC)
                    if s0 >= 1:
                        pe.wait_ge(exp_done, s * U + (u + 1 - U))
                    pe.matmul(s_ps[u][:], ident_bf[:], mask[:], start=True, stop=False)
                    for j in range(J):
                        h = u * J + j
                        m = pe.matmul(s_ps[u][:, j * T:(j + 1) * T], k_stack[buf][:, h, tok], q_stack[buf][:, h, tok],
                                      start=False, stop=(j == J - 1))
                    m.then_inc(scores_ready, 1)

                def attend(u):
                    if u == 0:
                        pe.wait_ge(v_pad_ready, s)
                        if s0 >= 2:
                            pe.wait_ge(x2_ready, s - 1)
                    for j in range(J):
                        m = pe.matmul(o_ps[32 * j:32 * j + 32, :], v_pad[1 - p][:, u * T + 32 * j:u * T + 32 * j + 32],
                                      probs[1 - p][:, u * J + j, :], start=(u == 0), stop=(u == U - 1))
                    if u == U - 1:
                        m.then_inc(pv_done, 1)

                def fc(c):
                    f = group_of(s, s0, 3)
                    if c == 0:
                        pe.wait_ge(xn2_t_ready, f + 1)
                        if s0 >= 5:
                            pe.wait_ge(spike_op_done, f * SPIKE_OPS + (1 - SPIKE_OPS))
                    if c == 2 and s0 >= 5:
                        pe.wait_ge(relu_ready, f * 2)
                    m = pe.matmul(f_ps[c // 2][:, (c % 2) * G * T:(c % 2 + 1) * G * T], wfc[:, c * 128:(c + 1) * 128],
                                  xn2_t[:], start=True, stop=True)
                    if c % 2 == 1:
                        m.then_inc(fc_done, 1)

                def proj(c):
                    f = group_of(s, s0, 4)
                    if c % 2 == 0:
                        pe.wait_ge(hidden_ready, f * 2 + (c // 2 + 1))
                    m = pe.matmul(f_ps[0][:, 0:G * T], wproj[:, c, :], hidden[:, c // 2, (c % 2) * G * T:(c % 2 + 1) * G * T],
                                  start=(c == 0), stop=(c == FF // 128 - 1))
                    if c == FF // 128 - 1:
                        m.then_inc(proj_done, 1)

                if on["scores"]:
                    scores(0)
                    scores(1)
                    scores(2)
                if on["turn"]:
                    pe.wait_ge(xn2_ready, s - 1)
                    if p == 0 and s0 >= 4:
                        pe.wait_ge(xn2_t_ready, group_of(s, s0, 2))
                    if p == 0 and s0 >= 8:
                        pe.wait_ge(result_ready, group_of(s, s0, 6))
                    pe.transpose(tr_ps[:, p * T:(p + 1) * T], xn2[:, p, :], ident[:]).then_inc(xn2_turned, 1)
                if on["attend"]:
                    attend(0)
                    attend(1)
                if on["finish"]:
                    f = group_of(s, s0, 7)
                    pe.wait_ge(spike_op_done, f * SPIKE_OPS + SPIKE_OPS)
                    if s0 <= B + 1:
                        pe.wait_ge(xn2_t_ready, group_of(s, s0, 3) + 1)
                    for k in range(G):
                        m = pe.transpose(count_ps[:, k * D:(k + 1) * D], count[:, k * T:(k + 1) * T], ident_bf[:])
                    m.then_inc(count_turned, 1)
                if on["scores"]:
                    scores(3)
                if on["attend"]:
                    attend(2)
                    attend(3)
                if on["fc"]:
                    fc(0)
                    fc(1)
                    fc(2)
                if on["proj"]:
                    proj(0)
                    proj(1)
                if on["attend"]:
                    pe.wait_ge(attn_t_ready, s)
                    pe.matmul(y_ps, attn_t[:], wc[:], start=True, stop=True).then_inc(y_ready, 1)
                if on["fc"]:
                    fc(3)
                if on["proj"]:
                    proj(2)
                    proj(3)

            stage2(pe, slot)

        @block.vector
        def _(dve):
            def moments_of(g, g0):
                p = g0 % 2
                if g0 >= 1:
                    dve.wait_ge(moments1_ready, g)
                dve.wait_ge(x_loaded[p], loads_of(g, p))
                settle(dve)
                for i in range(PG):
                    st = dve.bn_stats(stats1[:, i, :], x_all[:, bass.ds(g * PG + i, 1), :].squeeze(1)
                                      if not isinstance(g, int) else x_all[:, g * PG + i, :])
                st.then_inc(stats1_done, 1)
                if g0 >= 1:
                    dve.wait_ge(rstd1_ready, g)
                dve.wait_ge(stats1_done, g + 1)
                settle(dve)
                for i in range(PG):
                    ag = dve.bn_aggr(moments1[:, i, :], stats1[:, i, :])
                ag.then_inc(moments1_ready, 1)

            def normalise(g, g0):
                dve.wait_ge(moments1_ready, g + 1)
                dve.wait_ge(rstd1_ready, g + 1)
                if g0 >= 1:
                    dve.wait_ge(xn1_turned, g)
                for i in range(PG):
                    xs = x_all[:, g * PG + i, :] if isinstance(g, int) else x_all[:, bass.ds(g * PG + i, 1), :].squeeze(1)
                    n = dve.tensor_scalar(xn1[:, i, :], xs, moments1[:, i, 0:1], rstd1[:, i:i + 1], ALU.subtract, ALU.mult)
                n.then_inc(xn1_ready, 1)

            for t in k_stack:
                last = dve.memset(t[64:ROWS, :, :].rearrange("r h t -> r (h t)").bitcast(F32), 0.0)
            last.then_inc(zeroed, 1)
            moments_of(0, 0)
            normalise(0, 0)
            dve.wait_ge(consts_loaded, 16 * 12)
            dve.wait_ge(gates_ready, 1)
            dve.tensor_scalar(spike_gain[:], tanh_gates[:, 1:2], 1.0 / STEPS, None, ALU.mult).then_inc(gates_scaled, 1)
            dve.tensor_scalar(bc_row[:], bc_row[:], tanh_gates[:, 0:1], None, ALU.mult).then_inc(gates_scaled, 1)
            bv_b = bv_row[:].unsqueeze(1).to_broadcast([T, PG, D])

            def body(g, g0):
                p = g0 % 2
                if g0 < NPG - 1:
                    moments_of(g + 1, g0 + 1)
                dve.wait_ge(v_projected, g + 1)
                dve.tensor_tensor(v_all[:, bass.ds(g * PG, PG), :], v_ps[p][:].rearrange("p (b d) -> p b d", b=PG), bv_b,
                                  ALU.add).then_inc(v_ready, 1)
                if g0 < NPG - 1:
                    normalise(g + 1, g0 + 1)
                if g0 >= 1:
                    dve.wait_ge(q_split, g)
                dve.wait_ge(q_full_ready, g + 1)
                dve.tensor_tensor(q_rest[:], q_full[:, p, :], q_parts[:, p, 0, :], ALU.subtract).then_inc(q_rest_ready, 1)
                dve.wait_ge(q_rest_ready, g + 1)
                dve.tensor_copy(q_parts[:, p, 1, :], q_rest[:]).then_inc(q_mid_ready, 1)
                dve.wait_ge(q_mid_ready, g + 1)
                dve.tensor_tensor(q_parts[:, p, 2, :], q_rest[:], q_parts[:, p, 1, :], ALU.subtract).then_inc(q_split, 1)

            stage1(dve, body)
            dve.wait_ge(v_ready, NPG)
            dve.wait_ge(zeroed, 2)
            dve.wait_ge(gates_scaled, 2)

            def slot(s, s0):
                on = live(s0)
                p = s0 % 2

                def seq(b):
                    return x_all[:, b, :] if isinstance(b, int) else x_all[:, bass.ds(b, 1), :].squeeze(1)

                def maxes(u):
                    dve.wait_ge(scores_ready, s * U + (u + 1))
                    if u == 0 and s0 >= 2:
                        dve.wait_ge(exp_done, s * U - U)
                    dve.tensor_reduce(neg_max[:, p, u * J:(u + 1) * J], s_ps[u][:].rearrange("p (j q) -> p j q", j=J),
                                      AX_X, ALU.max, negate=True).then_inc(max_ready, 1)

                def spikes(ops):
                    f = group_of(s, s0, 5 if ops[0] == 0 else 6)
                    for n in ops:
                        done = f * SPIKE_OPS
                        if n == 0:
                            dve.wait_ge(proj_done, f + 1)
                            if s0 >= 7:
                                dve.wait_ge(spike_op_done, f * SPIKE_OPS)
                            op = dve.tensor_copy(y_t[:], f_ps[0][:, 0:G * T])
                        else:
                            dve.wait_ge(spike_op_done, done + n)
                            m = y_t if n <= 3 else mem
                            if n == 1:
                                if s0 >= 7:
                                    dve.wait_ge(count_turned, f)
                                op = dve.tensor_scalar(count[:], y_t[:], THRESHOLD, None, ALU.is_gt)
                            elif n % 3 == 2:
                                op = dve.scalar_tensor_tensor(out=charge[:], in0=m[:], scalar=BETA, in1=y_t[:],
                                                              op0=ALU.mult, op1=ALU.add)
                            elif n % 3 == 0:
                                op = dve.scalar_tensor_tensor(out=mem[:], in0=m[:], scalar=THRESHOLD, in1=charge[:],
                                                              op0=ALU.is_gt, op1=ALU.subtract, reverse1=True)
                            else:
                                op = dve.scalar_tensor_tensor(out=count[:], in0=mem[:], scalar=THRESHOLD, in1=count[:],
                                                              op0=ALU.is_gt, op1=ALU.add)
                        op.then_inc(spike_op_done, 1)

                if on["scores"]:
                    maxes(0)
                    maxes(1)
                    maxes(2)
                if on["attend"]:
                    dve.wait_ge(exp_done, s * U)
                    if s0 >= 2:
                        dve.wait_ge(v_pad_ready, s - 1)
                    dve.reciprocal(inv_sum[:], row_sum[:, 1 - p, :]).then_inc(inv_ready, 1)
                    dve.wait_ge(inv_ready, s)
                    if s0 >= 3:
                        dve.wait_ge(pv_done, s - 2)
                    vb = v_all[:, s - 1, :] if isinstance(s, int) else v_all[:, bass.ds(s - 1, 1), :].squeeze(1)
                    dst = v_pad[1 - p][:].rearrange("p (u r) -> p u r", u=U)[:, :, 0:T]\
                        .rearrange("p u (j c) -> p u j c", j=J)[:, :, :, 0:ND]
                    dve.tensor_tensor(dst, vb.rearrange("p (u j d) -> p u j d", u=U, j=J),
                                      inv_sum[:].rearrange("p (u j) -> p u j", u=U).unsqueeze(3).to_broadcast([T, U, J, ND]),
                                      ALU.mult).then_inc(v_pad_ready, 1)
                if on["turn"] and p == 1:
                    dve.wait_ge(xn2_turned, s - 1)
                    if s0 >= 5:
                        dve.wait_ge(fc_done, group_of(s, s0, 3) * 2)
                    dve.tensor_copy(xn2_t[:], tr_ps[:, 0:G * T]).then_inc(xn2_t_ready, 1)
                if on["scores"]:
                    maxes(3)
                if on["finish"]:
                    f = group_of(s, s0, 7)
                    dve.wait_ge(count_turned, f + 1)
                    xs = x_all[:, bass.ds(f * G, G), :]
                    dve.scalar_tensor_tensor(out=xs, in0=count_ps.rearrange("p (b d) -> p b d", b=G), scalar=spike_gain[:],
                                             in1=xs, op0=ALU.mult, op1=ALU.add).then_inc(result_ready, 1)
                if on["spikes_a"]:
                    spikes(range(0, 7))
                if on["spikes_b"]:
                    spikes(range(7, SPIKE_OPS))
                if on["attend"]:
                    dve.wait_ge(pv_done, s)
                    if s0 >= 2:
                        dve.wait_ge(y_ready, s - 1)
                    dve.tensor_copy(attn_t[:], o_ps).then_inc(attn_t_ready, 1)
                    dve.wait_ge(y_ready, s)
                    dve.wait_ge(bias_added, s)
                    xs = seq(s - 1)
                    dve.scalar_tensor_tensor(out=xs, in0=y_ps, scalar=tanh_gates[:, 0:1], in1=xs,
                                             op0=ALU.mult, op1=ALU.add).then_inc(x2_ready, 1)
                    if s0 >= 2:
                        dve.wait_ge(moments2_ready, s - 1)
                    dve.wait_ge(x2_ready, s)
                    settle(dve)
                    dve.bn_stats(stats2[:], xs).then_inc(stats2_done, 1)
                    dve.wait_ge(stats2_done, s)
                    settle(dve)
                    dve.bn_aggr(moments2[:], stats2[:]).then_inc(moments2_ready, 1)
                if on["attend"]:
                    dve.wait_ge(moments2_ready, s)
                    dve.wait_ge(rstd2_ready, s)
                    if s0 >= 3:
                        dve.wait_ge(xn2_turned, s - 2)
                    dve.tensor_scalar(xn2[:, 1 - p, :], xs, moments2[:, 0:1], rstd2[:],
                                      ALU.subtract, ALU.mult).then_inc(xn2_ready, 1)

            stage2(dve, slot)


_OUT = ((B, T, D), "float32")


def kernel(x, ctx_1024, g_xattn, g_ffn, L0_xattn_Wq, L0_xattn_bq, L0_xattn_Wk, L0_xattn_bk, L0_xattn_Wv,
           L0_xattn_bv, L0_xattn_Wc, L0_xattn_bc, L0_ffn_W_fc, L0_ffn_W_proj):
    import numpy as np
    import concourse.bacc as bacc
    from concourse.bass_utils import run_bass_kernel_spmd

    def t(a):
        return np.ascontiguousarray(np.asarray(a).T)

    wc_rows = np.ascontiguousarray(t(L0_xattn_Wc).reshape(U, J, ND, D).transpose(1, 0, 2, 3).reshape(D, D))
    laid_out = dict(
        x=np.ascontiguousarray(x),
        ctxT=np.ascontiguousarray(np.asarray(ctx_1024).reshape(B * T, D).T),
        g_xattn=np.ascontiguousarray(g_xattn), g_ffn=np.ascontiguousarray(g_ffn),
        WqT=t(L0_xattn_Wq), bq=np.ascontiguousarray(L0_xattn_bq).reshape(D, 1),
        WkT=t(L0_xattn_Wk), bk=np.ascontiguousarray(L0_xattn_bk).reshape(D, 1),
        WvT=t(L0_xattn_Wv), bv=np.ascontiguousarray(L0_xattn_bv),
        WcT=wc_rows, bc=np.ascontiguousarray(L0_xattn_bc),
        WfcT=t(L0_ffn_W_fc), WprojT=t(L0_ffn_W_proj),
    )
    nc = bacc.Bacc("TRN2", target_bir_lowering=False, num_devices=1)
    arrays, args = {}, []
    for name, a in laid_out.items():
        arrays[f"in_{name}"] = a
        args.append(nc.dram_tensor(f"in_{name}", a.shape, mybir.dt.from_np(a.dtype), kind="ExternalInput").ap())
    args.append(nc.dram_tensor("out_0", _OUT[0], mybir.dt.from_np(np.dtype(_OUT[1])), kind="ExternalOutput").ap())
    gated_block_kernel(nc, *args)
    r = run_bass_kernel_spmd(nc, [arrays], core_ids=[0])
    return r.results[0]["out_0"]
```

```python
from contextlib import ExitStack

import concourse.bass as bass
from concourse import mybir

ALU = mybir.AluOpType
ACT = mybir.ActivationFunctionType
AX_X = mybir.AxisListType.X
F32 = mybir.dt.float32
BF16 = mybir.dt.bfloat16

B = 32
T = 128
D = 128
H = 16
ND = D // H
FF = 4 * D
EPS = 1e-5
SCALE = float(ND) ** -0.5
MASKED = -1e30
BETA = 0.9
THRESHOLD = 1.0
STEPS = 5

PG = 4
NPG = B // PG
G = 2
NG = B // G
U = 4
J = H // U
PARTS = 3
TURN = PARTS * ND
ROWS = 96
STACK_INC = 16 * 2 * PARTS
SPIKE_OPS = 1 + 2 * (STEPS - 1)
VP = T + ND
assert PARTS * TURN <= ROWS


def gated_block_kernel(nc, x, ctxT, g_xattn, g_ffn, WqT, bq, WkT, bk, WvT, bv, WcT, bc, WfcT, WprojT, out):
    with ExitStack() as ctx:
        def sb(name, shape, dt=F32):
            return ctx.enter_context(nc.sbuf_tensor(name, shape, dt))

        def pb(name):
            return ctx.enter_context(nc.psum_tensor(name, [128, 512], F32))

        def sem(name):
            return ctx.enter_context(nc.semaphore(name))

        wq = sb("wq", [D, D])
        wk = sb("wk", [D, D])
        wv = sb("wv", [D, D])
        wc = sb("wc", [D, D])
        wfc = sb("wfc", [D, FF])
        wproj = sb("wproj", [128, FF // 128, D])
        bq_col = sb("bq_col", [D, 1])
        bq_scaled = sb("bq_scaled", [D, 1])
        bk_col = sb("bk_col", [D, 1])
        bv_row = sb("bv_row", [128, D])
        bc_row = sb("bc_row", [128, D])
        gates = sb("gates", [128, 2])
        tanh_gates = sb("tanh_gates", [128, 2])
        spike_gain = sb("spike_gain", [128, 1])
        ident = sb("ident", [128, 128])
        ident_bf = sb("ident_bf", [128, 128], BF16)
        mask = sb("mask", [T, J * T], BF16)
        minus_half = sb("minus_half", [128, PG])
        eps = sb("eps", [128, PG])
        idle = sb("idle", [128, 1])

        x_all = sb("x_all", [T, B, D])
        v_all = sb("v_all", [T, B, D])

        ctx_t = sb("ctx_t", [D, 2, PG * T])
        stats1 = sb("stats1", [T, PG, 6])
        moments1 = sb("moments1", [T, PG, 2])
        var_eps1 = sb("var_eps1", [T, PG])
        rstd1 = sb("rstd1", [T, PG])
        xn1 = sb("xn1", [T, PG, D])
        xn1_t = sb("xn1_t", [D, PG * T])
        q_parts = sb("q_parts", [D, 2, PARTS, PG * T], BF16)
        k_parts = sb("k_parts", [D, 2, PARTS, PG * T], BF16)
        q_full = sb("q_full", [D, 2, PG * T])
        k_full = sb("k_full", [D, 2, PG * T])
        q_rest = sb("q_rest", [D, PG * T])
        k_rest = sb("k_rest", [D, PG * T])

        q_stack = [sb(f"q_stack{i}", [ROWS, H, G * T], BF16) for i in range(2)]
        k_stack = [sb(f"k_stack{i}", [ROWS, H, G * T], BF16) for i in range(2)]
        probs = [sb(f"probs{i}", [T, H, T]) for i in range(2)]
        neg_max = sb("neg_max", [T, 2, H])
        row_sum = sb("row_sum", [T, 2, H])
        inv_sum = sb("inv_sum", [T, H])
        v_pad = [sb(f"v_pad{i}", [T, U * VP]) for i in range(2)]
        attn_t = sb("attn_t", [D, T])
        stats2 = sb("stats2", [T, 6])
        moments2 = sb("moments2", [T, 2])
        var_eps2 = sb("var_eps2", [T, 1])
        rstd2 = sb("rstd2", [T, 1])
        xn2 = sb("xn2", [T, 2, D])
        xn2_t = sb("xn2_t", [D, G * T])
        relu = sb("relu", [128, 2, 2 * G * T])
        hidden = sb("hidden", [128, 2, 2 * G * T])
        y_t = sb("y_t", [D, G * T])
        mem = [y_t] + [sb(f"mem{t}", [D, G * T]) for t in range(1, STEPS)]
        charge = sb("charge", [D, G * T])
        spikes = sb("spikes", [D, STEPS, G * T], BF16)

        q_dram = nc.dram_tensor("q_dram", [PARTS, D, B * T], BF16).ap()
        k_dram = nc.dram_tensor("k_dram", [2 * PARTS - 1, D, B * T], BF16).ap()

        bank = [pb(f"bank{i}") for i in range(8)]
        k_ps, q_ps, v_ps, t_ps = bank[0:2], bank[2:4], bank[4:6], bank[6:8]
        s_ps = bank[0:4]
        o_ps = bank[4][:, 0:T]
        y_ps = bank[4][:, 128:128 + D]
        tr_ps = bank[5]
        f_ps = bank[6:8]
        count_ps = tr_ps[:, G * T:G * T + G * D]

        consts_loaded = sem("consts_loaded")
        x_loaded = [sem(f"x_loaded{i}") for i in range(2)]
        ctx_loaded = [sem(f"ctx_loaded{i}") for i in range(2)]
        zeroed = sem("zeroed")
        tables_ready = sem("tables_ready")
        filled = sem("filled")
        gates_ready = sem("gates_ready")
        gates_scaled = sem("gates_scaled")
        bq_ready = sem("bq_ready")
        stats1_done = sem("stats1_done")
        moments1_ready = sem("moments1_ready")
        var_eps1_ready = sem("var_eps1_ready")
        rstd1_ready = sem("rstd1_ready")
        xn1_ready = sem("xn1_ready")
        xn1_turned = sem("xn1_turned")
        xn1_t_ready = sem("xn1_t_ready")
        k_projected = sem("k_projected")
        q_projected = sem("q_projected")
        v_projected = sem("v_projected")
        k_full_ready = sem("k_full_ready")
        q_full_ready = sem("q_full_ready")
        v_ready = sem("v_ready")
        q_rest_ready = sem("q_rest_ready")
        q_mid_ready = sem("q_mid_ready")
        q_split = sem("q_split")
        k_rest_ready = sem("k_rest_ready")
        k_split = sem("k_split")
        parts_stored = [sem(f"parts_stored{i}") for i in range(2)]
        stack_loaded = [sem(f"stack_loaded{i}") for i in range(2)]
        scores_ready = sem("scores_ready")
        max_ready = sem("max_ready")
        exp_done = sem("exp_done")
        inv_ready = sem("inv_ready")
        v_pad_ready = sem("v_pad_ready")
        pv_done = sem("pv_done")
        attn_t_ready = sem("attn_t_ready")
        y_ready = sem("y_ready")
        bias_added = sem("bias_added")
        x2_ready = sem("x2_ready")
        stats2_done = sem("stats2_done")
        moments2_ready = sem("moments2_ready")
        var_eps2_ready = sem("var_eps2_ready")
        rstd2_ready = sem("rstd2_ready")
        xn2_ready = sem("xn2_ready")
        xn2_turned = sem("xn2_turned")
        xn2_t_ready = sem("xn2_t_ready")
        fc_done = sem("fc_done")
        relu_ready = sem("relu_ready")
        hidden_ready = sem("hidden_ready")
        proj_done = sem("proj_done")
        spike_op_done = sem("spike_op_done")
        spikes_ready = sem("spikes_ready")
        counted = sem("counted")
        result_ready = sem("result_ready")
        stored = sem("stored")

        x_tok = x.rearrange("b t d -> t b d")
        out_tok = out.rearrange("b t d -> t b d")
        STORE_INC = 16 * 3

        def stage1(eng, body):
            body(0, 0)
            body(1, 1)
            with eng.Fori(0, (NPG - 4) // 2) as t:
                body(t * 2 + 2, 2)
                body(t * 2 + 3, 3)
            body(NPG - 2, NPG - 2)
            body(NPG - 1, NPG - 1)

        def stage2(eng, body):
            first, tail, last = 8, B - 4, B + 7
            for s in range(first):
                body(s, s)
            with eng.Fori(0, (tail - first) // 4) as t:
                for i in range(4):
                    body(t * 4 + (first + i), first + i)
            for s in range(tail, last):
                body(s, s)

        def loads_of(g, p):
            return 16 * (g // 2 + 1) if isinstance(g, int) else (g - p) * 8 + 16

        def stored_before(g, g0):
            return STORE_INC * (g // 2) if isinstance(g, int) else (g - g0 % 2) * (STORE_INC // 2)

        def live(s0):
            odd = s0 % 2 == 1
            return dict(
                scores=s0 < B,
                next_scores=s0 + 1 < B,
                attend=1 <= s0 <= B,
                turn=2 <= s0 <= B + 1,
                fc=not odd and 4 <= s0 <= B + 2,
                proj=odd and 5 <= s0 <= B + 3,
                spikes_a=not odd and 6 <= s0 <= B + 4,
                spikes_b=odd and 7 <= s0 <= B + 5,
                finish=not odd and 8 <= s0 <= B + 6,
            )

        def group_of(s, s0, lag):
            if isinstance(s, int):
                return (s - lag) // 2
            return ((s - s0) // 2) + (s0 - lag) // 2

        def settle(dve):
            dve.memset(idle[:], 0.0)

        block = ctx.enter_context(nc.Block())

        @block.sync
        def _(sp):
            def load(g, g0):
                p = g0 % 2
                if g0 >= 2:
                    sp.wait_ge(moments1_ready, g - 1)
                sp.dma_start(x_all[:, bass.ds(g * PG, PG), :], x_tok[:, bass.ds(g * PG, PG), :]).then_inc(x_loaded[p], 16)
                if g0 >= 2:
                    sp.wait_ge(k_projected, g - 1)
                    sp.wait_ge(v_projected, g - 1)
                sp.dma_start(ctx_t[:, p, :], ctxT[:, bass.ds(g * (PG * T), PG * T)]).then_inc(ctx_loaded[p], 16)

            def keep_parts(g, g0):
                p = g0 % 2
                tok = bass.ds(g * (PG * T), PG * T)
                sp.wait_ge(k_split, g + 1)
                for first, n in ((0, PARTS), (PARTS, PARTS - 1)):
                    sp.dma_start(k_dram[first:first + n, :, tok].rearrange("s r t -> r s t"),
                                 k_parts[:, p, 0:n, :]).then_inc(parts_stored[p], 16)
                sp.wait_ge(q_split, g + 1)
                sp.dma_start(q_dram[:, :, tok].rearrange("s r t -> r s t"), q_parts[:, p, :, :]).then_inc(parts_stored[p], 16)

            def stack(g, g0):
                p = g0 % 2
                if g0 >= 2:
                    sp.wait_ge(scores_ready, g * (G * U) - G * U)
                for r in range(PARTS):
                    rows = slice(r * TURN, (r + 1) * TURN)
                    for dst, dram, first in ((k_stack, k_dram, r), (q_stack, q_dram, 0)):
                        src = dram[first:first + PARTS, :, bass.ds(g * (G * T), G * T)]\
                            .rearrange("s (d h) t -> (s d) h t", h=H)
                        sp.dma_start(dst[p][rows, :, :], src).then_inc(stack_loaded[p], 16)

            load(0, 0)
            load(1, 1)

            def body(g, g0):
                if g0 < NPG - 2:
                    load(g + 2, g0 + 2)
                keep_parts(g, g0)
                if g0 == 0:
                    sp.wait_ge(parts_stored[0], STORE_INC)
                    sp.wait_ge(zeroed, 2)
                    stack(0, 0)
                    stack(1, 1)

            stage1(sp, body)
            for p in range(2):
                sp.wait_ge(parts_stored[p], STORE_INC * NPG // 2)

            LAG = 5

            def store(f):
                sp.dma_start(out_tok[:, bass.ds(f * G, G), :], x_all[:, bass.ds(f * G, G), :]).then_inc(stored, 16)

            for g in range(2, LAG + 1):
                stack(g, g)
            sp.wait_ge(result_ready, 1)
            store(0)
            with sp.Fori(0, (NG - LAG - 1) // 2) as t:
                for i in range(2):
                    stack(t * 2 + (LAG + 1 + i), LAG + 1 + i)
                    sp.wait_ge(result_ready, t * 2 + (i + 2))
                    store(t * 2 + (i + 1))
            for f in range(NG - LAG, NG):
                sp.wait_ge(result_ready, f + 1)
                store(f)
            sp.wait_ge(stored, 16 * NG)

        @block.scalar
        def _(act):
            for dst, src in (
                (gates[:, 0:1], g_xattn.partition_broadcast(128)), (gates[:, 1:2], g_ffn.partition_broadcast(128)),
                (wk[:], WkT), (bk_col[:], bk), (wv[:], WvT), (wq[:], WqT), (bq_col[:], bq),
                (bv_row[:], bv.partition_broadcast(128)), (bc_row[:], bc.partition_broadcast(128)),
                (wc[:], WcT), (wfc[:], WfcT),
            ):
                act.dma_start(dst, src).then_inc(consts_loaded, 16)
            act.dma_start(wproj[:], WprojT.rearrange("(c f) d -> f c d", f=128)).then_inc(consts_loaded, 16)
            act.wait_ge(consts_loaded, 16 * 12)
            act.activation(tanh_gates[:], gates[:], ACT.Tanh).then_inc(gates_ready, 1)
            act.mul(bq_scaled[:], bq_col[:], SCALE).then_inc(bq_ready, 1)
            act.wait_ge(bq_ready, 1)

            def turn_evac(g):
                act.wait_ge(xn1_turned, g + 1)
                act.activation(xn1_t[:], t_ps[0][:], ACT.Copy).then_inc(xn1_t_ready, 1)

            turn_evac(0)

            def body(g, g0):
                p = g0 % 2
                act.wait_ge(k_projected, g + 1)
                if g0 >= 2:
                    act.wait_ge(k_split, g - 1)
                    act.wait_ge(parts_stored[p], stored_before(g, g0))
                act.activation(k_full[:, p, :], k_ps[p][:], ACT.Identity, bias=bk_col[:])
                act.activation(k_parts[:, p, 0, :], k_ps[p][:], ACT.Identity, bias=bk_col[:]).then_inc(k_full_ready, 1)
                act.wait_ge(q_projected, g + 1)
                if g0 >= 2:
                    act.wait_ge(q_split, g - 1)
                act.activation(q_full[:, p, :], q_ps[p][:], ACT.Identity, bias=bq_scaled[:], scale=SCALE)
                act.activation(q_parts[:, p, 0, :], q_ps[p][:], ACT.Identity, bias=bq_scaled[:], scale=SCALE).then_inc(q_full_ready, 1)
                if g0 < NPG - 1:
                    turn_evac(g + 1)

            stage1(act, body)

            def slot(s, s0):
                on = live(s0)
                p = s0 % 2

                def exps(u):
                    act.wait_ge(max_ready, s * U + (u + 1))
                    for j in range(J):
                        h = u * J + j
                        e = act.activation(probs[p][:, h, :], s_ps[u][:, j * T:(j + 1) * T], ACT.Exp,
                                           bias=neg_max[:, p, h:h + 1], accum_out=row_sum[:, p, h:h + 1])
                    e.then_inc(exp_done, 1)

                def relus(half):
                    f = group_of(s, s0, 4 + half)
                    act.wait_ge(fc_done, f * 2 + (half + 1))
                    if s0 >= 6:
                        act.wait_ge(hidden_ready, f * 2 + (half - 1))
                    act.activation(relu[:, half, :], f_ps[half][:], ACT.Relu).then_inc(relu_ready, 1)

                if on["scores"]:
                    if s0 >= 2:
                        act.wait_ge(pv_done, s - 1)
                        act.wait_ge(inv_ready, s - 1)
                    exps(0)
                if on["proj"]:
                    relus(1)
                if on["scores"]:
                    exps(1)
                if on["fc"]:
                    relus(0)
                if on["scores"]:
                    exps(2)
                    exps(3)

            stage2(act, slot)

        @block.gpsimd
        def _(pool):
            pool.memset(ident[:], 0.0)
            pool.memset(ident_bf[:], 0.0)
            pool.memset(minus_half[:], -0.5)
            pool.memset(eps[:], EPS)
            pool.memset(mask[:], 0.0).then_inc(filled, 1)
            pool.wait_ge(filled, 1)
            for t in (ident, ident_bf):
                pool.affine_select(out=t[:], in_=t[:], compare_op=ALU.not_equal, fill=1.0, base=0,
                                   pattern=[[-1, 128]], channel_multiplier=1)
            mask_v = mask[:].rearrange("p (j q) -> p j q", j=J)
            pool.affine_select(out=mask_v, in_=mask_v, compare_op=ALU.is_ge, fill=MASKED, base=0,
                               pattern=[[0, J], [1, T]], channel_multiplier=-1).then_inc(tables_ready, 1)

            def rstd1_of(g, g0):
                if g0 >= 1:
                    pool.wait_ge(rstd1_ready, g)
                    pool.wait_ge(xn1_ready, g)
                pool.wait_ge(moments1_ready, g + 1)
                pool.tensor_tensor(var_eps1[:], moments1[:, :, 1], eps[:], ALU.add).then_inc(var_eps1_ready, 1)
                pool.wait_ge(var_eps1_ready, g + 1)
                pool.tensor_tensor(rstd1[:], var_eps1[:], minus_half[:], ALU.pow).then_inc(rstd1_ready, 1)

            for t in q_stack:
                pool.memset(t[:].rearrange("r h t -> r (h t)").bitcast(F32), 0.0)
            rstd1_of(0, 0)
            for t in v_pad:
                last = pool.memset(t[:], 0.0)
            last.then_inc(zeroed, 1)

            def body(g, g0):
                p = g0 % 2
                if g0 < NPG - 1:
                    rstd1_of(g + 1, g0 + 1)
                pool.wait_ge(k_full_ready, g + 1)
                if g0 >= 1:
                    pool.wait_ge(k_split, g)
                pool.tensor_tensor(k_rest[:], k_full[:, p, :], k_parts[:, p, 0, :], ALU.subtract)
                pool.tensor_tensor(k_parts[:, p, 1, :], k_full[:, p, :], k_parts[:, p, 0, :], ALU.subtract).then_inc(k_rest_ready, 1)
                pool.wait_ge(k_rest_ready, g + 1)
                pool.tensor_tensor(k_parts[:, p, 2, :], k_rest[:], k_parts[:, p, 1, :], ALU.subtract).then_inc(k_split, 1)

            stage1(pool, body)

            def slot(s, s0):
                on = live(s0)
                if on["scores"]:
                    if s0 == 0:
                        pool.wait_ge(gates_scaled, 2)
                        pool.wait_ge(xn1_ready, NPG)
                    xs = x_all[:, s, :] if isinstance(s, int) else x_all[:, bass.ds(s, 1), :].squeeze(1)
                    pool.tensor_tensor(xs, xs, bc_row[:], ALU.add).then_inc(bias_added, 1)
                if on["turn"]:
                    if s0 >= 3:
                        pool.wait_ge(rstd2_ready, s - 2)
                        pool.wait_ge(xn2_ready, s - 2)
                    pool.wait_ge(moments2_ready, s - 1)
                    pool.tensor_tensor(var_eps2[:], moments2[:, 1:2], eps[:, 0:1], ALU.add).then_inc(var_eps2_ready, 1)
                    pool.wait_ge(var_eps2_ready, s - 1)
                    pool.tensor_tensor(rstd2[:], var_eps2[:], minus_half[:, 0:1], ALU.pow).then_inc(rstd2_ready, 1)

                def square(half):
                    f = group_of(s, s0, 4 + half)
                    pool.wait_ge(relu_ready, f * 2 + (half + 1))
                    if s0 >= 6 and half == 0:
                        pool.wait_ge(proj_done, f)
                    pool.tensor_tensor(hidden[:, half, :], relu[:, half, :], relu[:, half, :], ALU.mult)\
                        .then_inc(hidden_ready, 1)

                if on["proj"]:
                    square(1)
                if on["fc"]:
                    square(0)

            stage2(pool, slot)

        @block.tensor
        def _(pe):
            pe.wait_ge(tables_ready, 1)
            pe.wait_ge(consts_loaded, 16 * 12)

            def turn(g):
                pe.wait_ge(xn1_ready, g + 1)
                for i in range(PG):
                    t = pe.transpose(t_ps[0][:, i * T:(i + 1) * T], xn1[:, i, :], ident[:])
                t.then_inc(xn1_turned, 1)

            turn(0)

            def body(g, g0):
                p = g0 % 2
                pe.wait_ge(ctx_loaded[p], loads_of(g, p))
                if g0 >= 2:
                    pe.wait_ge(k_full_ready, g - 1)
                pe.matmul(k_ps[p][:], wk[:], ctx_t[:, p, :], start=True, stop=True).then_inc(k_projected, 1)
                pe.wait_ge(xn1_t_ready, g + 1)
                if g0 >= 2:
                    pe.wait_ge(q_full_ready, g - 1)
                pe.matmul(q_ps[p][:], wq[:], xn1_t[:], start=True, stop=True).then_inc(q_projected, 1)
                if g0 >= 2:
                    pe.wait_ge(v_ready, g - 1)
                for i in range(PG):
                    m = pe.matmul(v_ps[p][:, i * D:(i + 1) * D], ctx_t[:, p, i * T:(i + 1) * T], wv[:], start=True, stop=True)
                m.then_inc(v_projected, 1)
                if g0 < NPG - 1:
                    turn(g + 1)

            stage1(pe, body)

            pe.wait_ge(zeroed, 2)
            pe.wait_ge(k_full_ready, NPG)
            pe.wait_ge(q_full_ready, NPG)
            pe.wait_ge(v_ready, NPG)

            def scores(u, b, b0):
                buf, i = (b0 // G) % 2, b0 % G
                tok = slice(i * T, (i + 1) * T)
                if u == 0 and i == 0:
                    pe.wait_ge(stack_loaded[buf], ((b - b0) // 4 + (b0 // 4 + 1)) * STACK_INC)
                if b0 >= 1:
                    pe.wait_ge(exp_done, b * U + (u + 1 - U))
                pe.matmul(s_ps[u][:], ident_bf[:], mask[:], start=True, stop=False)
                for j in range(J):
                    h = u * J + j
                    m = pe.matmul(s_ps[u][:, j * T:(j + 1) * T], k_stack[buf][:, h, tok], q_stack[buf][:, h, tok],
                                  start=False, stop=(j == J - 1))
                m.then_inc(scores_ready, 1)

            scores(0, 0, 0)
            scores(1, 0, 0)

            def slot(s, s0):
                on = live(s0)
                p = s0 % 2

                def attend(u):
                    if u == 0:
                        pe.wait_ge(v_pad_ready, s)
                        if s0 >= 2:
                            pe.wait_ge(x2_ready, s - 1)
                    for j in range(J):
                        m = pe.matmul(o_ps[32 * j:32 * j + 32, :], v_pad[1 - p][:, u * T + 32 * j:u * T + 32 * j + 32],
                                      probs[1 - p][:, u * J + j, :], start=(u == 0), stop=(u == U - 1))
                    if u == U - 1:
                        m.then_inc(pv_done, 1)

                def fc(c):
                    f = group_of(s, s0, 4)
                    if c == 0:
                        pe.wait_ge(xn2_t_ready, f + 1)
                        if s0 >= 6:
                            pe.wait_ge(spike_op_done, f * SPIKE_OPS + (1 - SPIKE_OPS))
                    if c == 2 and s0 >= 6:
                        pe.wait_ge(relu_ready, f * 2)
                    m = pe.matmul(f_ps[c // 2][:, (c % 2) * G * T:(c % 2 + 1) * G * T], wfc[:, c * 128:(c + 1) * 128],
                                  xn2_t[:], start=True, stop=True)
                    if c % 2 == 1:
                        m.then_inc(fc_done, 1)

                def proj(c):
                    f = group_of(s, s0, 5)
                    if c % 2 == 0:
                        pe.wait_ge(hidden_ready, f * 2 + (c // 2 + 1))
                    m = pe.matmul(f_ps[0][:, 0:G * T], wproj[:, c, :], hidden[:, c // 2, (c % 2) * G * T:(c % 2 + 1) * G * T],
                                  start=(c == 0), stop=(c == FF // 128 - 1))
                    if c == FF // 128 - 1:
                        m.then_inc(proj_done, 1)

                if on["scores"]:
                    scores(2, s, s0)
                if on["finish"]:
                    f = group_of(s, s0, 8)
                    pe.wait_ge(spikes_ready, f * STEPS + STEPS)
                    if s0 <= B + 2:
                        pe.wait_ge(xn2_t_ready, group_of(s, s0, 4) + 1)
                    for i in range(G):
                        for t in range(STEPS):
                            m = pe.matmul(count_ps[:, i * D:(i + 1) * D], spikes[:, t, i * T:(i + 1) * T], ident_bf[:],
                                          start=(t == 0), stop=(t == STEPS - 1))
                    m.then_inc(counted, 1)
                if on["fc"]:
                    fc(0)
                    fc(1)
                if on["proj"]:
                    proj(0)
                    proj(1)
                if on["scores"]:
                    scores(3, s, s0)
                if on["attend"]:
                    attend(0)
                    attend(1)
                if on["next_scores"]:
                    scores(0, s + 1, s0 + 1)
                if on["attend"]:
                    attend(2)
                    attend(3)
                if on["next_scores"]:
                    scores(1, s + 1, s0 + 1)
                if on["turn"]:
                    pe.wait_ge(xn2_ready, s - 1)
                    if p == 0 and s0 >= 4:
                        pe.wait_ge(xn2_t_ready, group_of(s, s0, 2))
                    if p == 0 and s0 >= 8:
                        pe.wait_ge(result_ready, group_of(s, s0, 8) + 1)
                    pe.transpose(tr_ps[:, p * T:(p + 1) * T], xn2[:, p, :], ident[:]).then_inc(xn2_turned, 1)
                if on["attend"]:
                    pe.wait_ge(attn_t_ready, s)
                    pe.matmul(y_ps, attn_t[:], wc[:], start=True, stop=True).then_inc(y_ready, 1)
                if on["fc"]:
                    fc(2)
                    fc(3)
                if on["proj"]:
                    proj(2)
                    proj(3)

            stage2(pe, slot)

        @block.vector
        def _(dve):
            def moments_of(g, g0):
                p = g0 % 2
                if g0 >= 1:
                    dve.wait_ge(moments1_ready, g)
                dve.wait_ge(x_loaded[p], loads_of(g, p))
                settle(dve)
                for i in range(PG):
                    st = dve.bn_stats(stats1[:, i, :], x_all[:, bass.ds(g * PG + i, 1), :].squeeze(1)
                                      if not isinstance(g, int) else x_all[:, g * PG + i, :])
                st.then_inc(stats1_done, 1)
                if g0 >= 1:
                    dve.wait_ge(rstd1_ready, g)
                dve.wait_ge(stats1_done, g + 1)
                settle(dve)
                for i in range(PG):
                    ag = dve.bn_aggr(moments1[:, i, :], stats1[:, i, :])
                ag.then_inc(moments1_ready, 1)

            def normalise(g, g0):
                dve.wait_ge(moments1_ready, g + 1)
                dve.wait_ge(rstd1_ready, g + 1)
                if g0 >= 1:
                    dve.wait_ge(xn1_turned, g)
                for i in range(PG):
                    xs = x_all[:, g * PG + i, :] if isinstance(g, int) else x_all[:, bass.ds(g * PG + i, 1), :].squeeze(1)
                    n = dve.tensor_scalar(xn1[:, i, :], xs, moments1[:, i, 0:1], rstd1[:, i:i + 1], ALU.subtract, ALU.mult)
                n.then_inc(xn1_ready, 1)

            for t in k_stack:
                last = dve.memset(t[64:ROWS, :, :].rearrange("r h t -> r (h t)").bitcast(F32), 0.0)
            last.then_inc(zeroed, 1)
            moments_of(0, 0)
            normalise(0, 0)
            dve.wait_ge(consts_loaded, 16 * 12)
            dve.wait_ge(gates_ready, 1)
            dve.tensor_scalar(spike_gain[:], tanh_gates[:, 1:2], 1.0 / STEPS, None, ALU.mult).then_inc(gates_scaled, 1)
            dve.tensor_scalar(bc_row[:], bc_row[:], tanh_gates[:, 0:1], None, ALU.mult).then_inc(gates_scaled, 1)
            bv_b = bv_row[:].unsqueeze(1).to_broadcast([T, PG, D])

            def body(g, g0):
                p = g0 % 2
                if g0 < NPG - 1:
                    moments_of(g + 1, g0 + 1)
                dve.wait_ge(v_projected, g + 1)
                dve.tensor_tensor(v_all[:, bass.ds(g * PG, PG), :], v_ps[p][:].rearrange("p (b d) -> p b d", b=PG), bv_b,
                                  ALU.add).then_inc(v_ready, 1)
                if g0 < NPG - 1:
                    normalise(g + 1, g0 + 1)
                if g0 >= 1:
                    dve.wait_ge(q_split, g)
                dve.wait_ge(q_full_ready, g + 1)
                dve.tensor_tensor(q_rest[:], q_full[:, p, :], q_parts[:, p, 0, :], ALU.subtract).then_inc(q_rest_ready, 1)
                dve.wait_ge(q_rest_ready, g + 1)
                dve.tensor_copy(q_parts[:, p, 1, :], q_rest[:]).then_inc(q_mid_ready, 1)
                dve.wait_ge(q_mid_ready, g + 1)
                dve.tensor_tensor(q_parts[:, p, 2, :], q_rest[:], q_parts[:, p, 1, :], ALU.subtract).then_inc(q_split, 1)

            stage1(dve, body)
            dve.wait_ge(v_ready, NPG)
            dve.wait_ge(zeroed, 2)
            dve.wait_ge(gates_scaled, 2)

            def maxes(u, b, b0):
                dve.wait_ge(scores_ready, b * U + (u + 1))
                if u == 0 and b0 >= 2:
                    dve.wait_ge(exp_done, b * U - U)
                dve.tensor_reduce(neg_max[:, b0 % 2, u * J:(u + 1) * J], s_ps[u][:].rearrange("p (j q) -> p j q", j=J),
                                  AX_X, ALU.max, negate=True).then_inc(max_ready, 1)

            maxes(0, 0, 0)
            maxes(1, 0, 0)

            def slot(s, s0):
                on = live(s0)
                p = s0 % 2

                def seq(b):
                    return x_all[:, b, :] if isinstance(b, int) else x_all[:, bass.ds(b, 1), :].squeeze(1)

                def spike_ops(ops):
                    if not (on["spikes_a"] or on["spikes_b"]):
                        return
                    f = group_of(s, s0, 6 if on["spikes_a"] else 7)
                    for n in ops:
                        if n == 0:
                            dve.wait_ge(proj_done, f + 1)
                            if s0 >= 8:
                                dve.wait_ge(spike_op_done, f * SPIKE_OPS)
                            op = dve.tensor_copy(y_t[:], f_ps[0][:, 0:G * T])
                        else:
                            before, after = mem[(n - 1) // 2], mem[(n + 1) // 2]
                            dve.wait_ge(spike_op_done, f * SPIKE_OPS + n)
                            if n % 2:
                                op = dve.scalar_tensor_tensor(out=charge[:], in0=before[:], scalar=BETA, in1=y_t[:],
                                                              op0=ALU.mult, op1=ALU.add)
                            else:
                                op = dve.scalar_tensor_tensor(out=mem[n // 2][:], in0=before[:], scalar=THRESHOLD,
                                                              in1=charge[:], op0=ALU.is_gt, op1=ALU.subtract, reverse1=True)
                        op.then_inc(spike_op_done, 1)
                        if n % 2 or n == SPIKE_OPS - 1:
                            t = n // 2
                            if t == 0 and s0 >= 8:
                                dve.wait_ge(counted, f)
                            if n == SPIKE_OPS - 1:
                                dve.wait_ge(spike_op_done, f * SPIKE_OPS + SPIKE_OPS)
                            dve.tensor_scalar(spikes[:, t, :], mem[t][:], THRESHOLD, None, ALU.is_gt)\
                                .then_inc(spikes_ready, 1)

                first_op = 1 if on["spikes_a"] else 5
                if on["spikes_a"]:
                    spike_ops([0])
                if on["scores"]:
                    maxes(2, s, s0)
                if on["attend"]:
                    dve.wait_ge(exp_done, s * U)
                    if s0 >= 2:
                        dve.wait_ge(v_pad_ready, s - 1)
                    dve.reciprocal(inv_sum[:], row_sum[:, 1 - p, :]).then_inc(inv_ready, 1)
                if on["turn"]:
                    dve.wait_ge(rstd2_ready, s - 1)
                    if s0 >= 4:
                        dve.wait_ge(xn2_turned, s - 3)
                    dve.tensor_scalar(xn2[:, p, :], seq(s - 2), moments2[:, 0:1], rstd2[:],
                                      ALU.subtract, ALU.mult).then_inc(xn2_ready, 1)
                if on["attend"]:
                    dve.wait_ge(inv_ready, s)
                    if s0 >= 3:
                        dve.wait_ge(pv_done, s - 2)
                    dst = v_pad[1 - p][:].rearrange("p (u r) -> p u r", u=U)[:, :, 0:T]\
                        .rearrange("p u (j c) -> p u j c", j=J)[:, :, :, 0:ND]
                    vb = v_all[:, s - 1, :] if isinstance(s, int) else v_all[:, bass.ds(s - 1, 1), :].squeeze(1)
                    dve.tensor_tensor(dst, vb.rearrange("p (u j d) -> p u j d", u=U, j=J),
                                      inv_sum[:].rearrange("p (u j) -> p u j", u=U).unsqueeze(3).to_broadcast([T, U, J, ND]),
                                      ALU.mult).then_inc(v_pad_ready, 1)
                if on["finish"]:
                    f = group_of(s, s0, 8)
                    dve.wait_ge(counted, f + 1)
                    xs = x_all[:, bass.ds(f * G, G), :]
                    dve.scalar_tensor_tensor(out=xs, in0=count_ps.rearrange("p (b d) -> p b d", b=G), scalar=spike_gain[:],
                                             in1=xs, op0=ALU.mult, op1=ALU.add).then_inc(result_ready, 1)
                spike_ops([first_op])
                if on["scores"]:
                    maxes(3, s, s0)
                spike_ops([first_op + 1])
                if on["next_scores"]:
                    maxes(0, s + 1, s0 + 1)
                if on["attend"]:
                    dve.wait_ge(pv_done, s)
                    if s0 >= 2:
                        dve.wait_ge(y_ready, s - 1)
                    dve.tensor_copy(attn_t[:], o_ps).then_inc(attn_t_ready, 1)
                spike_ops([first_op + 2])
                if on["next_scores"]:
                    maxes(1, s + 1, s0 + 1)
                if on["attend"]:
                    dve.wait_ge(y_ready, s)
                    dve.wait_ge(bias_added, s)
                    xs = seq(s - 1)
                    dve.scalar_tensor_tensor(out=xs, in0=y_ps, scalar=tanh_gates[:, 0:1], in1=xs,
                                             op0=ALU.mult, op1=ALU.add).then_inc(x2_ready, 1)
                    if s0 >= 2:
                        dve.wait_ge(moments2_ready, s - 1)
                    dve.wait_ge(x2_ready, s)
                    settle(dve)
                    dve.bn_stats(stats2[:], xs).then_inc(stats2_done, 1)
                if on["turn"] and p == 1:
                    dve.wait_ge(xn2_turned, s - 1)
                    if s0 >= 5:
                        dve.wait_ge(fc_done, group_of(s, s0, 3) * 2)
                    dve.tensor_copy(xn2_t[:], tr_ps[:, 0:G * T]).then_inc(xn2_t_ready, 1)
                if on["attend"]:
                    dve.wait_ge(stats2_done, s)
                    settle(dve)
                    dve.bn_aggr(moments2[:], stats2[:]).then_inc(moments2_ready, 1)
                spike_ops([first_op + 3])

            stage2(dve, slot)


_OUT = ((B, T, D), "float32")


def kernel(x, ctx_1024, g_xattn, g_ffn, L0_xattn_Wq, L0_xattn_bq, L0_xattn_Wk, L0_xattn_bk, L0_xattn_Wv,
           L0_xattn_bv, L0_xattn_Wc, L0_xattn_bc, L0_ffn_W_fc, L0_ffn_W_proj):
    import numpy as np
    import concourse.bacc as bacc
    from concourse.bass_utils import run_bass_kernel_spmd

    def t(a):
        return np.ascontiguousarray(np.asarray(a).T)

    def by_dim(a):
        return np.ascontiguousarray(np.asarray(a).reshape(H, ND, -1).transpose(1, 0, 2).reshape(D, -1))

    wc_rows = np.ascontiguousarray(t(L0_xattn_Wc).reshape(U, J, ND, D).transpose(1, 0, 2, 3).reshape(D, D))
    laid_out = dict(
        x=np.ascontiguousarray(x),
        ctxT=np.ascontiguousarray(np.asarray(ctx_1024).reshape(B * T, D).T),
        g_xattn=np.ascontiguousarray(g_xattn), g_ffn=np.ascontiguousarray(g_ffn),
        WqT=t(by_dim(L0_xattn_Wq)), bq=by_dim(L0_xattn_bq),
        WkT=t(by_dim(L0_xattn_Wk)), bk=by_dim(L0_xattn_bk),
        WvT=t(L0_xattn_Wv), bv=np.ascontiguousarray(L0_xattn_bv),
        WcT=wc_rows, bc=np.ascontiguousarray(L0_xattn_bc),
        WfcT=t(L0_ffn_W_fc), WprojT=t(L0_ffn_W_proj),
    )
    nc = bacc.Bacc("TRN2", target_bir_lowering=False, num_devices=1)
    arrays, args = {}, []
    for name, a in laid_out.items():
        arrays[f"in_{name}"] = a
        args.append(nc.dram_tensor(f"in_{name}", a.shape, mybir.dt.from_np(a.dtype), kind="ExternalInput").ap())
    args.append(nc.dram_tensor("out_0", _OUT[0], mybir.dt.from_np(np.dtype(_OUT[1])), kind="ExternalOutput").ap())
    gated_block_kernel(nc, *args)
    r = run_bass_kernel_spmd(nc, [arrays], core_ids=[0])
    return r.results[0]["out_0"]
```

```python
from contextlib import ExitStack

import concourse.bass as bass
from concourse import mybir

ALU = mybir.AluOpType
ACT = mybir.ActivationFunctionType
AX_X = mybir.AxisListType.X
F32 = mybir.dt.float32
BF16 = mybir.dt.bfloat16

B = 32
T = 128
D = 128
H = 16
ND = D // H
FF = 4 * D
EPS = 1e-5
SCALE = float(ND) ** -0.5
MASKED = -1e30
BETA = 0.9
THRESHOLD = 1.0
STEPS = 5

PG = 4
NPG = B // PG
G = 2
NG = B // G
HALF = T // 2
PAIRS = H // 2
U = 3
LOWS = PAIRS // 2
TILES = 4
BANKS = 4
PARTS = 3
TURN = PARTS * ND
ROWS = 96
STACK_INC = 16 * 2 * PARTS
SPIKE_OPS = 1 + 2 * (STEPS - 1)
VP = 32
assert PARTS * TURN <= ROWS


def gated_block_kernel(nc, x, ctxT, w_qkv, vectors, w_late, out):
    with ExitStack() as ctx:
        def sb(name, shape, dt=F32):
            return ctx.enter_context(nc.sbuf_tensor(name, shape, dt))

        def pb(name):
            return ctx.enter_context(nc.psum_tensor(name, [128, 512], F32))

        def sem(name):
            return ctx.enter_context(nc.semaphore(name))

        qkv_sb = sb("qkv_sb", [D, 3 * D + 2])
        wk, wq, wv = (qkv_sb[:, i * D:(i + 1) * D] for i in range(3))
        bk_col, bq_col = (qkv_sb[:, 3 * D + i:3 * D + i + 1] for i in range(2))
        late_sb = sb("late_sb", [128, D + FF + FF])
        wc, wfc = late_sb[:, 0:D], late_sb[:, D:D + FF]
        wproj = late_sb[:, D + FF:].rearrange("p (c d) -> p c d", d=D)
        vectors_sb = sb("vectors_sb", [128, 2 * D + 2])
        bv_row, bc_row, gates = vectors_sb[:, 0:D], vectors_sb[:, D:2 * D], vectors_sb[:, 2 * D:]
        bq_scaled = sb("bq_scaled", [D, 1])
        tanh_gates = sb("tanh_gates", [128, 2])
        spike_gain = sb("spike_gain", [128, 1])
        ident = sb("ident", [128, 128])
        ident_bf = sb("ident_bf", [128, 128], BF16)
        low_mask = sb("low_mask", [T, LOWS * T], BF16)
        high_mask = sb("high_mask", [T, PAIRS * HALF], BF16)
        head_here = sb("head_here", [T, 2, 2])
        minus_half = sb("minus_half", [128, PG])
        eps = sb("eps", [128, PG])
        zero_col = sb("zero_col", [128, 1])
        idle = sb("idle", [128, 1])

        x_all = sb("x_all", [T, B, D])
        v_all = sb("v_all", [T, B, D])

        ctx_t = sb("ctx_t", [D, 2, PG * T])
        stats1 = sb("stats1", [T, PG, 6])
        moments1 = sb("moments1", [T, 2, PG, 2])
        var_eps1 = sb("var_eps1", [T, PG])
        rstd1 = sb("rstd1", [T, 2, PG])
        xn1 = sb("xn1", [T, PG, D])
        xn1_t = sb("xn1_t", [D, PG * T])
        q_parts = sb("q_parts", [D, PARTS, B * T], BF16)
        k_parts = sb("k_parts", [D, PARTS, B * T], BF16)
        q_full = sb("q_full", [D, 2, PG * T])
        k_full = sb("k_full", [D, 2, PG * T])
        q_rest = sb("q_rest", [D, PG * T])
        k_rest = sb("k_rest", [D, PG * T])

        q_stack = [sb(f"q_stack{i}", [ROWS, H, G * T], BF16) for i in range(2)]
        k_stack = [sb(f"k_stack{i}", [ROWS, H, G * T], BF16) for i in range(2)]
        probs = [sb(f"probs{i}", [T, PAIRS * (T + HALF)]) for i in range(2)]
        neg_max = sb("neg_max", [T, 2, H])
        row_sum = sb("row_sum", [T, 2, H])
        inv_row = sb("inv_row", [T, H])
        inv_sum = sb("inv_sum", [T, 2, PAIRS, 2])
        v_pad = [sb(f"v_pad{i}", [T, 2 * PAIRS * VP + VP // 2]) for i in range(2)]
        attn_t = sb("attn_t", [D, T])
        stats2 = sb("stats2", [T, 6])
        moments2 = sb("moments2", [T, 2])
        var_eps2 = sb("var_eps2", [T, 1])
        rstd2 = sb("rstd2", [T, 1])
        centred = sb("centred", [T, D])
        xn2 = sb("xn2", [T, 2, D])
        xn2_t = sb("xn2_t", [D, G * T])
        relu = sb("relu", [128, 2, 2 * G * T])
        hidden = sb("hidden", [128, 2, 2 * G * T])
        y_t = sb("y_t", [D, G * T])
        mem = [y_t] + [sb(f"mem{t}", [D, G * T]) for t in range(1, STEPS)]
        charge = sb("charge", [D, G * T])
        spikes = [sb(f"spikes{i}", [D, STEPS, G * T], BF16) for i in range(2)]

        q_dram = nc.dram_tensor("q_dram", [PARTS, D, B * T], BF16).ap()
        k_dram = nc.dram_tensor("k_dram", [2 * PARTS - 1, D, B * T], BF16).ap()

        bank = [pb(f"bank{i}") for i in range(8)]
        k_ps, q_ps, v_ps, t_ps = bank[0:2], bank[2:4], bank[4:6], bank[6:8]
        s_ps = bank[0:BANKS]
        o_ps = bank[4][:, 0:T]
        y_ps = bank[4][:, 128:128 + D]
        tr_ps = bank[5]
        f_ps = bank[6:8]
        count_ps = tr_ps[:, G * T:G * T + G * D]

        qkv_loaded = sem("qkv_loaded")
        vectors_loaded = sem("vectors_loaded")
        late_loaded = sem("late_loaded")
        x_loaded = [sem(f"x_loaded{i}") for i in range(3)]
        ctx_loaded = [sem(f"ctx_loaded{i}") for i in range(2)]
        column_zeroed = sem("column_zeroed")
        k_stacks_zeroed = sem("k_stacks_zeroed")
        q_stack0_zeroed = sem("q_stack0_zeroed")
        q_stack1_zeroed = sem("q_stack1_zeroed")
        v_pad_zeroed = sem("v_pad_zeroed")
        ident_ready = sem("ident_ready")
        masks_ready = sem("masks_ready")
        filled = sem("filled")
        gates_ready = sem("gates_ready")
        gates_scaled = sem("gates_scaled")
        bq_ready = sem("bq_ready")
        stats1_done = sem("stats1_done")
        moments1_ready = sem("moments1_ready")
        var_eps1_ready = sem("var_eps1_ready")
        rstd1_ready = sem("rstd1_ready")
        xn1_ready = sem("xn1_ready")
        xn1_turned = sem("xn1_turned")
        xn1_t_ready = sem("xn1_t_ready")
        k_projected = sem("k_projected")
        q_projected = sem("q_projected")
        v_projected = sem("v_projected")
        k_full_ready = sem("k_full_ready")
        q_full_ready = sem("q_full_ready")
        v_ready = sem("v_ready")
        q_rest_ready = sem("q_rest_ready")
        q_mid_ready = sem("q_mid_ready")
        q_split = sem("q_split")
        k_rest_ready = sem("k_rest_ready")
        k_mid_ready = sem("k_mid_ready")
        k_split = sem("k_split")
        parts_stored = [sem(f"parts_stored{i}") for i in range(2)]
        stack_loaded = [sem(f"stack_loaded{i}") for i in range(2)]
        scores_ready = sem("scores_ready")
        max_ready = sem("max_ready")
        exp_done = sem("exp_done")
        inv_row_ready = sem("inv_row_ready")
        inv_ready = sem("inv_ready")
        v_pad_ready = sem("v_pad_ready")
        pv_done = sem("pv_done")
        attn_t_ready = sem("attn_t_ready")
        y_ready = sem("y_ready")
        bias_added = sem("bias_added")
        x2_ready = sem("x2_ready")
        stats2_done = sem("stats2_done")
        moments2_ready = sem("moments2_ready")
        var_eps2_ready = sem("var_eps2_ready")
        rstd2_ready = sem("rstd2_ready")
        centred_ready = sem("centred_ready")
        xn2_ready = sem("xn2_ready")
        xn2_turned = sem("xn2_turned")
        xn2_t_ready = sem("xn2_t_ready")
        fc_done = sem("fc_done")
        relu_ready = [sem(f"relu_ready{i}") for i in range(2)]
        late_relu_ready = sem("late_relu_ready")
        hidden_ready = sem("hidden_ready")
        late_hidden_ready = sem("late_hidden_ready")
        proj_done = sem("proj_done")
        spike_op_done = sem("spike_op_done")
        spikes_ready = sem("spikes_ready")
        late_spikes_ready = sem("late_spikes_ready")
        counted = sem("counted")
        result_ready = sem("result_ready")
        stored = sem("stored")

        x_tok = x.rearrange("b t d -> t b d")
        out_tok = out.rearrange("b t d -> t b d")
        STORE_INC = 16 * 3

        def stage1(eng, body):
            body(0, 0)
            with eng.Fori(0, (NPG - 4) // 2) as t:
                body(t * 2 + 1, 1)
                body(t * 2 + 2, 2)
            for g in range(NPG - 3, NPG):
                body(g, g)

        def stage2(eng, body):
            first, tail, last = 8, B - 4, B + 7
            for s in range(first):
                body(s, s)
            with eng.Fori(0, (tail - first) // 4) as t:
                for i in range(4):
                    body(t * 4 + (first + i), first + i)
            for s in range(tail, last):
                body(s, s)

        def loads_of(g, p):
            return 16 * (g // 2 + 1) if isinstance(g, int) else (g - p) * 8 + 16

        def part(t, g, i):
            return t[:, i, bass.ds(g * (PG * T), PG * T)]

        def live(s0):
            odd = s0 % 2 == 1
            return dict(
                scores=s0 < B,
                next_scores=s0 + 1 < B,
                attend=1 <= s0 <= B,
                turn=2 <= s0 <= B + 1,
                fc=not odd and 4 <= s0 <= B + 2,
                proj=odd and 5 <= s0 <= B + 3,
                spikes_a=not odd and 6 <= s0 <= B + 4,
                spikes_b=odd and 7 <= s0 <= B + 5,
                finish=9 <= s0 <= B + 1 if odd else B + 2 <= s0 <= B + 6,
            )

        LATE = (B - 6) // 2

        def late_spikes(f, steps):
            return (f - LATE) * (STEPS - 1) + steps

        def spikes_by_dve(f, steps):
            return LATE * STEPS + (f - LATE) + steps

        def group_of(s, s0, lag):
            if isinstance(s, int):
                return (s - lag) // 2
            return ((s - s0) // 2) + (s0 - lag) // 2

        def fc_ps(s0):
            return s_ps[0:2] if s0 >= B + 2 else f_ps

        def scores_of(u, b0):
            return s_ps[(b0 * U + u) % BANKS]

        def score_block(t, u, i):
            return t[:, i * T:(i + 1) * T] if u < 2 else t[:, i * HALF:(i + 1) * HALF]

        def blocks_of(u):
            return LOWS if u < 2 else PAIRS

        def prob(t, high, pair):
            start = PAIRS * T + pair * HALF if high else pair * T
            return t[:, start:start + (HALF if high else T)]

        def v_of(b):
            return v_all[:, b, :] if isinstance(b, int) else v_all[:, bass.ds(b, 1), :].squeeze(1)

        def seq(b):
            return x_all[:, b, :] if isinstance(b, int) else x_all[:, bass.ds(b, 1), :].squeeze(1)

        def settle(dve):
            dve.memset(idle[:], 0.0)

        block = ctx.enter_context(nc.Block())

        @block.sync
        def _(sp):
            def load_ctx(g):
                sp.dma_start(ctx_t[:, g, :], ctxT[:, g * PG * T:(g + 1) * PG * T]).then_inc(ctx_loaded[g], 16)

            def load_x(first, n, loaded):
                b = slice(first * PG, (first + n) * PG)
                sp.dma_start(x_all[:, b, :], x_tok[:, b, :]).then_inc(loaded, 16)

            def keep_parts(g, g0):
                kept = parts_stored[min(g0, 1)]
                tok = bass.ds(g * (PG * T), PG * T)
                sp.wait_ge(q_split, g + 1)
                sp.wait_ge(k_split, g + 1)
                for first, n in ((0, PARTS), (PARTS, PARTS - 1)):
                    sp.dma_start(k_dram[first:first + n, :, tok].rearrange("s r t -> r s t"),
                                 k_parts[:, 0:n, tok]).then_inc(kept, 16)
                sp.dma_start(q_dram[:, :, tok].rearrange("s r t -> r s t"), q_parts[:, :, tok]).then_inc(kept, 16)

            def stack(g, g0):
                p = g0 % 2
                if g0 >= 2:
                    sp.wait_ge(scores_ready, g * (G * U) - G * U)
                for r in range(PARTS):
                    rows = slice(r * TURN, (r + 1) * TURN)
                    for dst, dram, first in ((k_stack, k_dram, r), (q_stack, q_dram, 0)):
                        src = dram[first:first + PARTS, :, bass.ds(g * (G * T), G * T)]\
                            .rearrange("s (d h) t -> (s d) h t", h=H)
                        sp.dma_start(dst[p][rows, :, :], src).then_inc(stack_loaded[p], 16)

            load_x(0, 1, x_loaded[0])
            load_ctx(0)
            load_x(1, 1, x_loaded[1])
            load_ctx(1)
            load_x(2, NPG - 2, x_loaded[2])
            sp.dma_start(late_sb[:], w_late).then_inc(late_loaded, 16)

            keep_parts(0, 0)
            with sp.Fori(0, (NPG - 4) // 2) as t:
                for i in range(2):
                    keep_parts(t * 2 + (1 + i), 1 + i)
            sp.wait_ge(parts_stored[0], STORE_INC)
            sp.wait_ge(k_stacks_zeroed, 2)
            sp.wait_ge(q_stack0_zeroed, 1)
            stack(0, 0)
            keep_parts(NPG - 3, NPG - 3)
            sp.wait_ge(q_stack1_zeroed, 1)
            stack(1, 1)
            for g in range(NPG - 2, NPG):
                keep_parts(g, g)
            sp.wait_ge(parts_stored[1], STORE_INC * (NPG - 1))

            LAG = 5

            def store(f):
                sp.dma_start(out_tok[:, bass.ds(f * G, G), :], x_all[:, bass.ds(f * G, G), :]).then_inc(stored, 16)

            for g in range(2, LAG + 1):
                stack(g, g)
            sp.wait_ge(result_ready, 1)
            store(0)
            with sp.Fori(0, (NG - LAG - 1) // 2) as t:
                for i in range(2):
                    stack(t * 2 + (LAG + 1 + i), LAG + 1 + i)
                    sp.wait_ge(result_ready, t * 2 + (i + 2))
                    store(t * 2 + (i + 1))
            for f in range(NG - LAG, NG):
                sp.wait_ge(result_ready, f + 1)
                store(f)
            sp.wait_ge(stored, 16 * NG)

        @block.scalar
        def _(act):
            act.dma_start(qkv_sb[:], w_qkv).then_inc(qkv_loaded, 16)
            act.dma_start(vectors_sb[:], vectors.partition_broadcast(128)).then_inc(vectors_loaded, 16)

            def zero_k_stack(i):
                rows = k_stack[i][64:ROWS, :, :].rearrange("r h t -> r (h t)").bitcast(F32)
                act.activation(rows, zero_col[64:ROWS, :].to_broadcast([ROWS - 64, H * G * T // 2]), ACT.Copy)\
                    .then_inc(k_stacks_zeroed, 1)

            act.wait_ge(column_zeroed, 1)
            zero_k_stack(0)
            act.wait_ge(qkv_loaded, 16)
            act.wait_ge(vectors_loaded, 16)
            act.activation(tanh_gates[:], gates, ACT.Tanh).then_inc(gates_ready, 1)
            act.mul(bq_scaled[:], bq_col, SCALE).then_inc(bq_ready, 1)
            act.wait_ge(bq_ready, 1)

            def turn_evac(g):
                act.wait_ge(xn1_turned, g + 1)
                act.activation(xn1_t[:], t_ps[0][:], ACT.Copy).then_inc(xn1_t_ready, 1)

            def q_mid(g):
                act.wait_ge(q_rest_ready, g + 1)
                act.activation(part(q_parts, g, 1), q_rest[:], ACT.Copy).then_inc(q_mid_ready, 1)

            def body(g, g0):
                p = g0 % 2
                act.wait_ge(k_projected, g + 1)
                if g0 >= 1:
                    act.wait_ge(k_split, g - 1)
                act.activation(k_full[:, p, :], k_ps[p][:], ACT.Identity, bias=bk_col)
                act.activation(part(k_parts, g, 0), k_ps[p][:], ACT.Identity, bias=bk_col).then_inc(k_full_ready, 1)
                if g0 == 0:
                    turn_evac(0)
                    zero_k_stack(1)
                act.wait_ge(q_projected, g + 1)
                if g0 >= 1:
                    act.wait_ge(q_split, g - 1)
                act.activation(q_full[:, p, :], q_ps[p][:], ACT.Identity, bias=bq_scaled[:], scale=SCALE)
                act.activation(part(q_parts, g, 0), q_ps[p][:], ACT.Identity, bias=bq_scaled[:], scale=SCALE)\
                    .then_inc(q_full_ready, 1)
                act.wait_ge(k_rest_ready, g + 1)
                act.activation(part(k_parts, g, 1), k_rest[:], ACT.Copy).then_inc(k_mid_ready, 1)
                if g0 < NPG - 1:
                    turn_evac(g + 1)
                if g0 < NPG - 1:
                    q_mid(g)
                if g0 < NPG - 2:
                    act.wait_ge(v_projected, g + 1)
                    act.dma_start(ctx_t[:, p, :], ctxT[:, bass.ds(g * (PG * T) + 2 * PG * T, PG * T)])\
                        .then_inc(ctx_loaded[p], 16)

            stage1(act, body)

            def slot(s, s0):
                on = live(s0)
                p = s0 % 2

                def exps(u):
                    act.wait_ge(max_ready, s * U + (u + 1))
                    for i in range(blocks_of(u)):
                        c = u * LOWS + i
                        e = act.activation(prob(probs[p], u == 2, c % PAIRS), score_block(scores_of(u, s0), u, i), ACT.Exp,
                                           bias=neg_max[:, p, c:c + 1], accum_out=row_sum[:, p, c:c + 1])
                    e.then_inc(exp_done, 1)

                def relus(half):
                    f = group_of(s, s0, 4 + p)
                    act.wait_ge(fc_done, f * 2 + (half + 1))
                    if s0 >= B + 2:
                        act.wait_ge(late_hidden_ready, s0 - B - 1)
                    elif s0 >= 7:
                        act.wait_ge(hidden_ready, f * 2 + (half - 1))
                    act.activation(relu[:, half, :], fc_ps(s0)[half][:], ACT.Relu)\
                        .then_inc(late_relu_ready if s0 >= B else relu_ready[0], 1)
                    if s0 >= B:
                        act.wait_ge(late_relu_ready, s0 - B + 1)
                        act.wait_ge(proj_done, f)
                        act.activation(hidden[:, half, :], relu[:, half, :], ACT.Square).then_inc(late_hidden_ready, 1)

                def turn_evac(lag):
                    f = group_of(s, s0, lag)
                    act.wait_ge(xn2_turned, f * G + G)
                    if s0 - lag >= G:
                        act.wait_ge(fc_done, f * 2)
                    act.activation(xn2_t[:], tr_ps[:, 0:G * T], ACT.Copy).then_inc(xn2_t_ready, 1)

                if on["scores"]:
                    if s0 >= 2:
                        act.wait_ge(pv_done, s - 1)
                        act.wait_ge(inv_row_ready, s - 1)
                    exps(0)
                    if s0 == 0:
                        q_mid(NPG - 1)
                if on["proj"]:
                    if s0 < B:
                        relus(0)
                    else:
                        relus(1)
                if on["scores"]:
                    exps(1)
                if on["fc"] and s0 <= B:
                    turn_evac(4)
                if on["scores"]:
                    exps(2)
                if on["fc"] and s0 >= B:
                    relus(0)
                if s0 == B + 1:
                    turn_evac(3)

            stage2(act, slot)

        @block.gpsimd
        def _(pool):
            pool.memset(zero_col[:], 0.0).then_inc(column_zeroed, 1)
            pool.memset(ident[:], 0.0)
            pool.memset(ident_bf[:], 0.0)
            pool.memset(minus_half[:], -0.5)
            pool.memset(eps[:], EPS)
            pool.memset(low_mask[:], 0.0)
            pool.memset(high_mask[:], 0.0).then_inc(filled, 1)
            pool.wait_ge(filled, 1)
            for t in (ident, ident_bf):
                last = pool.affine_select(out=t[:], in_=t[:], compare_op=ALU.not_equal, fill=1.0, base=0,
                                          pattern=[[-1, 128]], channel_multiplier=1)
            last.then_inc(ident_ready, 1)
            for t in v_pad:
                last = pool.memset(t[:], 0.0)
            last.then_inc(v_pad_zeroed, 1)

            def rstd1_of(g, g0):
                if g0 >= 1:
                    pool.wait_ge(rstd1_ready, g)
                if g0 >= 2:
                    pool.wait_ge(xn1_ready, g - 1)
                pool.wait_ge(moments1_ready, g + 1)
                pool.tensor_tensor(var_eps1[:], moments1[:, g0 % 2, :, 1], eps[:], ALU.add).then_inc(var_eps1_ready, 1)
                pool.wait_ge(var_eps1_ready, g + 1)
                pool.tensor_tensor(rstd1[:, g0 % 2, :], var_eps1[:], minus_half[:], ALU.pow).then_inc(rstd1_ready, 1)

            rstd1_of(0, 0)
            for first_step in (True, False):
                rows, base = (T, HALF) if first_step else (HALF, 0)
                for t, w in ((low_mask, T), (high_mask, HALF)):
                    m = t[0:rows, :].rearrange("p (j q) -> p j q", q=w)
                    f = pool.affine_select(out=m, in_=m, compare_op=ALU.is_ge, fill=MASKED, base=base,
                                           pattern=[[0, m.shape[1]], [1, w]], channel_multiplier=-1)
                if first_step:
                    f.then_inc(filled, 1)
                    pool.wait_ge(filled, 2)
                else:
                    f.then_inc(masks_ready, 1)
            rstd1_of(1, 1)

            def body(g, g0):
                p = g0 % 2
                if 0 < g0 < NPG - 2:
                    rstd1_of(g + 2, g0 + 2)
                pool.wait_ge(k_full_ready, g + 1)
                if g0 >= 1:
                    pool.wait_ge(k_split, g)
                pool.tensor_tensor(k_rest[:], k_full[:, p, :], part(k_parts, g, 0), ALU.subtract).then_inc(k_rest_ready, 1)
                if g0 == 0:
                    pool.memset(q_stack[0][:].rearrange("r h t -> r (h t)").bitcast(F32), 0.0).then_inc(q_stack0_zeroed, 1)
                    rstd1_of(2, 2)
                pool.wait_ge(k_mid_ready, g + 1)
                pool.tensor_tensor(part(k_parts, g, 2), k_rest[:], part(k_parts, g, 1), ALU.subtract).then_inc(k_split, 1)

            stage1(pool, body)

            def slot(s, s0):
                on = live(s0)
                p = s0 % 2
                if on["attend"]:
                    pool.wait_ge(inv_row_ready, s)
                    if s0 >= 2:
                        pool.wait_ge(v_pad_ready, s - 1)
                    pool.tensor_tensor(inv_sum[:], inv_row[:].rearrange("p (l r) -> p l r", l=2).unsqueeze(3)
                                       .to_broadcast([T, 2, PAIRS, 2]),
                                       head_here[:].unsqueeze(2).to_broadcast([T, 2, PAIRS, 2]), ALU.mult).then_inc(inv_ready, 1)
                    pool.wait_ge(inv_ready, s)
                    if s0 >= 3:
                        pool.wait_ge(pv_done, s - 2)
                    for high in range(2):
                        dst = v_pad[1 - p][:, high * PAIRS * VP:(high + 1) * PAIRS * VP]\
                            .rearrange("p (r c) -> p r c", c=VP)[:, :, VP // 2:].rearrange("p r (a d) -> p r a d", a=2)
                        vp = pool.tensor_tensor(dst, v_of(s - 1).rearrange("p (r a d) -> p r a d", a=2, d=ND),
                                                inv_sum[:, high, :, :].unsqueeze(3).to_broadcast([T, PAIRS, 2, ND]), ALU.mult)
                    vp.then_inc(v_pad_ready, 1)
                def square(half):
                    f = group_of(s, s0, 5)
                    pool.wait_ge(relu_ready[half], f + 1)
                    if s0 >= 7 and half == 0:
                        pool.wait_ge(proj_done, f)
                    pool.tensor_tensor(hidden[:, half, :], relu[:, half, :], relu[:, half, :], ALU.mult)\
                        .then_inc(hidden_ready, 1)

                if on["proj"] and s0 <= B:
                    square(0)
                if on["proj"] and s0 <= B:
                    square(1)
                if on["turn"]:
                    if s0 >= 3:
                        pool.wait_ge(xn2_ready, s - 2)
                    pool.wait_ge(moments2_ready, s - 1)
                    pool.tensor_tensor(var_eps2[:], moments2[:, 1:2], eps[:, 0:1], ALU.add).then_inc(var_eps2_ready, 1)
                    pool.wait_ge(var_eps2_ready, s - 1)
                    pool.tensor_tensor(rstd2[:], var_eps2[:], minus_half[:, 0:1], ALU.pow).then_inc(rstd2_ready, 1)
                    pool.tensor_tensor(centred[:], seq(s - 2), moments2[:, 0:1].to_broadcast([T, D]), ALU.subtract)\
                        .then_inc(centred_ready, 1)
                    pool.wait_ge(centred_ready, s - 1)
                    if s0 >= 4:
                        pool.wait_ge(xn2_turned, s - 3)
                    pool.wait_ge(rstd2_ready, s - 1)
                    pool.tensor_tensor(xn2[:, p, :], centred[:], rstd2[:].to_broadcast([T, D]), ALU.mult).then_inc(xn2_ready, 1)
                if s0 >= B and (on["spikes_a"] or on["spikes_b"]):
                    f = group_of(s, s0, 6 + p)
                    for t in ((2, 3) if p else (0, 1)):
                        if t == 0:
                            pool.wait_ge(counted, f - 1)
                        pool.wait_ge(spike_op_done, f * SPIKE_OPS + 2 * t + 1)
                        pool.tensor_scalar(spikes[f % 2][:, t, :], mem[t][:], THRESHOLD, None, ALU.is_gt)\
                            .then_inc(late_spikes_ready, 1)
                if on["scores"]:
                    if s0 == 0:
                        pool.wait_ge(gates_scaled, 2)
                        pool.wait_ge(xn1_ready, NPG)
                    pool.tensor_tensor(seq(s), seq(s), bc_row, ALU.add).then_inc(bias_added, 1)

            stage2(pool, slot)

        @block.tensor
        def _(pe):
            pe.wait_ge(qkv_loaded, 16)

            def turn(g):
                pe.wait_ge(xn1_ready, g + 1)
                for i in range(PG):
                    t = pe.transpose(t_ps[0][:, i * T:(i + 1) * T], xn1[:, i, :], ident[:])
                t.then_inc(xn1_turned, 1)

            def body(g, g0):
                p = g0 % 2
                pe.wait_ge(ctx_loaded[p], loads_of(g, p))
                if g0 >= 1:
                    pe.wait_ge(k_full_ready, g - 1)
                pe.matmul(k_ps[p][:], wk, ctx_t[:, p, :], start=True, stop=True).then_inc(k_projected, 1)
                if g0 == 0:
                    pe.wait_ge(ident_ready, 1)
                    turn(0)
                pe.wait_ge(xn1_t_ready, g + 1)
                if g0 >= 1:
                    pe.wait_ge(q_full_ready, g - 1)
                pe.matmul(q_ps[p][:], wq, xn1_t[:], start=True, stop=True).then_inc(q_projected, 1)
                if g0 == 0:
                    turn(1)
                if g0 >= 1:
                    pe.wait_ge(v_ready, g - 1)
                for i in range(PG):
                    for half in range(2):
                        for head, rows in ((0, half), (1, 1 - half)):
                            dst = v_ps[p][rows * HALF:(rows + 1) * HALF, i * D:(i + 1) * D]
                            m = pe.matmul(dst.rearrange("p (r a d) -> p r a d", a=2, d=ND)[:, :, head, :],
                                          ctx_t[:, p, i * T + half * HALF:i * T + (half + 1) * HALF],
                                          wv.rearrange("k (r a d) -> k r a d", a=2, d=ND)[:, :, head, :],
                                          start=True, stop=True)
                m.then_inc(v_projected, 1)
                if 0 < g0 < NPG - 1:
                    turn(g + 1)

            stage1(pe, body)

            def scores(u, b, b0):
                buf, i = (b0 // G) % 2, b0 % G
                at = i * T
                if u == 0 and i == 0:
                    pe.wait_ge(stack_loaded[buf], ((b - b0) // 4 + (b0 // 4 + 1)) * STACK_INC)
                if b0 * U + u >= BANKS:
                    pe.wait_ge(exp_done, b * U + (u + 1 - BANKS))
                ps = scores_of(u, b0)
                pe.matmul(ps[:], ident_bf[:], (low_mask if u < 2 else high_mask)[:], start=True, stop=False)
                for i in range(blocks_of(u)):
                    pair = (u * LOWS + i) % PAIRS
                    keys = (0, HALF) if u < 2 else (HALF, T)
                    for rows in range(2):
                        h = pair * 2 + (rows if u < 2 else 1 - rows)
                        m = pe.matmul(score_block(ps, u, i)[rows * HALF:(rows + 1) * HALF, :],
                                      k_stack[buf][:, h, at + keys[0]:at + keys[1]],
                                      q_stack[buf][:, h, at + keys[0]:at + T],
                                      start=False, stop=(i == blocks_of(u) - 1))
                m.then_inc(scores_ready, 1)

            pe.wait_ge(masks_ready, 1)
            pe.wait_ge(k_stacks_zeroed, 2)
            pe.wait_ge(q_stack0_zeroed, 1)
            pe.wait_ge(q_stack1_zeroed, 1)
            pe.wait_ge(k_full_ready, NPG)
            scores(0, 0, 0)
            scores(1, 0, 0)
            pe.wait_ge(q_full_ready, NPG)
            pe.wait_ge(v_ready, NPG)
            scores(2, 0, 0)
            scores(0, 1, 1)
            pe.wait_ge(late_loaded, 16)

            def slot(s, s0):
                on = live(s0)
                p = s0 % 2

                def attend(high):
                    if not high:
                        pe.wait_ge(v_pad_ready, s)
                        if s0 >= 2:
                            pe.wait_ge(x2_ready, s - 1)
                    for place in range(2):
                        for tile in range(TILES):
                            pair = place * TILES + tile
                            at = (high * PAIRS + pair) * VP + (0 if place else VP // 2)
                            m = pe.matmul(o_ps[32 * tile:32 * tile + 32, high * HALF:], v_pad[1 - p][:, at:at + 32],
                                          prob(probs[1 - p], high, pair), start=(not high and place == 0),
                                          stop=(high == 1 and place == 1))
                    if high:
                        m.then_inc(pv_done, 1)

                def fc(c):
                    f = group_of(s, s0, 4)
                    if c == 0:
                        pe.wait_ge(xn2_t_ready, f + 1)
                        if s0 == B + 2:
                            pe.wait_ge(exp_done, B * U)
                        elif s0 >= 6:
                            pe.wait_ge(spike_op_done, f * SPIKE_OPS + (1 - SPIKE_OPS))
                    if c == 2 and 6 <= s0 <= B:
                        pe.wait_ge(relu_ready[1], f)
                    m = pe.matmul(fc_ps(s0)[c // 2][:, (c % 2) * G * T:(c % 2 + 1) * G * T],
                                  wfc[:, c * 128:(c + 1) * 128], xn2_t[:], start=True, stop=True)
                    if c % 2 == 1:
                        m.then_inc(fc_done, 1)

                def proj(c):
                    f = group_of(s, s0, 5)
                    if s0 == B + 3 and c == 0:
                        pe.wait_ge(spike_op_done, f * SPIKE_OPS + (1 - SPIKE_OPS))
                    if s0 > B:
                        if c % 2 == 0:
                            pe.wait_ge(late_hidden_ready, s0 - B + c // 2)
                    elif c % 2 == 0:
                        pe.wait_ge(hidden_ready, f * 2 + (c // 2 + 1))
                    m = pe.matmul(f_ps[0][:, 0:G * T], wproj[:, c, :], hidden[:, c // 2, (c % 2) * G * T:(c % 2 + 1) * G * T],
                                  start=(c == 0), stop=(c == FF // 128 - 1))
                    if c == FF // 128 - 1:
                        m.then_inc(proj_done, 1)

                def ffn(first):
                    for c in (first, first + 1):
                        if on["fc"]:
                            fc(c)
                        if on["proj"]:
                            proj(c)

                def count():
                    f = group_of(s, s0, 9 if p else 8)
                    if s0 <= B + 2:
                        pe.wait_ge(xn2_t_ready, group_of(s, s0, 5 if p else 4) + 1)
                    if s0 >= 11:
                        pe.wait_ge(result_ready, f)
                    buf = spikes[(s0 - (9 if p else 8)) // 2 % 2]
                    for t in range(STEPS):
                        late = isinstance(f, int) and f >= LATE
                        if t in (0, STEPS - 1):
                            if not late:
                                pe.wait_ge(spikes_ready, f * STEPS + (t + 1 if t else STEPS - 1))
                            elif t == 0:
                                pe.wait_ge(late_spikes_ready, late_spikes(f, STEPS - 1))
                            else:
                                pe.wait_ge(spikes_ready, spikes_by_dve(f, 1))
                        for i in range(G):
                            m = pe.matmul(count_ps[:, i * D:(i + 1) * D], buf[:, t, i * T:(i + 1) * T], ident_bf[:],
                                          start=(t == 0 and i == 0), stop=(t == STEPS - 1 and i == G - 1))
                    m.then_inc(counted, 1)

                def turn_x2():
                    pe.wait_ge(xn2_ready, s - 1)
                    if p == 0 and s0 >= 4:
                        pe.wait_ge(xn2_t_ready, group_of(s, s0, 2))
                    if p == 1 and s0 >= 9:
                        pe.wait_ge(result_ready, group_of(s, s0, 9) + 1)
                    pe.transpose(tr_ps[:, p * T:(p + 1) * T], xn2[:, p, :], ident[:]).then_inc(xn2_turned, 1)

                if s0 < B + 2 and on["finish"]:
                    count()
                if s0 >= B:
                    ffn(0)
                if on["attend"]:
                    attend(0)
                    attend(1)
                if on["next_scores"]:
                    scores(1, s + 1, s0 + 1)
                if s0 < B:
                    ffn(0)
                if on["attend"]:
                    pe.wait_ge(attn_t_ready, s)
                    pe.matmul(y_ps, attn_t[:], wc, start=True, stop=True).then_inc(y_ready, 1)
                if s0 == B:
                    ffn(2)
                if on["next_scores"]:
                    scores(2, s + 1, s0 + 1)
                if on["turn"] and (s0 < B - 1 or s0 == B):
                    turn_x2()
                if s0 + 2 < B:
                    scores(0, s + 2, s0 + 2)
                if s0 != B:
                    ffn(2)
                if s0 in (B - 1, B + 1):
                    turn_x2()
                if s0 >= B + 2 and on["finish"]:
                    count()

            stage2(pe, slot)

        @block.vector
        def _(dve):
            def moments_of(g, g0):
                if g0 >= 1:
                    dve.wait_ge(moments1_ready, g)
                dve.wait_ge(x_loaded[min(g0, 2)], 16)
                settle(dve)
                for i in range(PG):
                    st = dve.bn_stats(stats1[:, i, :], x_all[:, bass.ds(g * PG + i, 1), :].squeeze(1)
                                      if not isinstance(g, int) else x_all[:, g * PG + i, :])
                st.then_inc(stats1_done, 1)
                if g0 >= 2:
                    dve.wait_ge(rstd1_ready, g - 1)
                dve.wait_ge(stats1_done, g + 1)
                settle(dve)
                for i in range(PG):
                    ag = dve.bn_aggr(moments1[:, g0 % 2, i, :], stats1[:, i, :])
                ag.then_inc(moments1_ready, 1)

            def normalise(g, g0):
                dve.wait_ge(moments1_ready, g + 1)
                dve.wait_ge(rstd1_ready, g + 1)
                if g0 >= 1:
                    dve.wait_ge(xn1_turned, g)
                for i in range(PG):
                    xs = x_all[:, g * PG + i, :] if isinstance(g, int) else x_all[:, bass.ds(g * PG + i, 1), :].squeeze(1)
                    n = dve.tensor_scalar(xn1[:, i, :], xs, moments1[:, g0 % 2, i, 0:1],
                                          rstd1[:, g0 % 2, i:i + 1], ALU.subtract, ALU.mult)
                n.then_inc(xn1_ready, 1)

            dve.memset(q_stack[1][64:ROWS, :, :].rearrange("r h t -> r (h t)").bitcast(F32), 0.0).then_inc(q_stack1_zeroed, 1)
            for rows in range(2):
                here = head_here[rows * HALF:(rows + 1) * HALF, :, :].rearrange("p l a -> p (l a)")
                dve.memset(here[:, 0:4:3], 1.0 - rows)
                dve.memset(here[:, 1:3], float(rows))
            moments_of(0, 0)
            normalise(0, 0)
            moments_of(1, 1)
            dve.wait_ge(vectors_loaded, 16)
            dve.wait_ge(gates_ready, 1)
            dve.tensor_scalar(spike_gain[:], tanh_gates[:, 1:2], 1.0 / STEPS, None, ALU.mult).then_inc(gates_scaled, 1)
            dve.tensor_scalar(bc_row, bc_row, tanh_gates[:, 0:1], None, ALU.mult).then_inc(gates_scaled, 1)

            def maxes(u, b, b0):
                dve.wait_ge(scores_ready, b * U + (u + 1))
                if u == 0 and b0 >= 2:
                    dve.wait_ge(exp_done, b * U - U)
                n = blocks_of(u)
                dve.tensor_reduce(neg_max[:, b0 % 2, u * LOWS:u * LOWS + n],
                                  scores_of(u, b0)[:].rearrange("p (j q) -> p j q", j=n), AX_X, ALU.max, negate=True)\
                    .then_inc(max_ready, 1)

            def q_last(g):
                dve.wait_ge(q_mid_ready, g + 1)
                dve.tensor_tensor(part(q_parts, g, 2), q_rest[:], part(q_parts, g, 1), ALU.subtract).then_inc(q_split, 1)

            bv_b = bv_row.unsqueeze(1).to_broadcast([T, PG, D])

            def body(g, g0):
                p = g0 % 2
                if g0 < NPG - 1:
                    normalise(g + 1, g0 + 1)
                if g0 == 0:
                    moments_of(2, 2)
                elif g0 < NPG - 3:
                    moments_of(g + 3, g0 + 3)
                if g0 == NPG - 1:
                    maxes(0, 0, 0)
                dve.wait_ge(q_full_ready, g + 1)
                if g0 >= 1:
                    dve.wait_ge(q_split, g)
                dve.tensor_tensor(q_rest[:], q_full[:, p, :], part(q_parts, g, 0), ALU.subtract).then_inc(q_rest_ready, 1)
                if g0 == 0:
                    moments_of(3, 3)
                dve.wait_ge(v_projected, g + 1)
                dve.tensor_tensor(v_all[:, bass.ds(g * PG, PG), :], v_ps[p][:].rearrange("p (b d) -> p b d", b=PG), bv_b,
                                  ALU.add).then_inc(v_ready, 1)
                if g0 == NPG - 1:
                    maxes(1, 0, 0)
                if g0 < NPG - 1:
                    q_last(g)

            stage1(dve, body)
            dve.wait_ge(v_ready, NPG)
            dve.wait_ge(v_pad_zeroed, 1)
            dve.wait_ge(gates_scaled, 2)

            def slot(s, s0):
                on = live(s0)
                p = s0 % 2

                spiking = on["spikes_a"] or on["spikes_b"]
                ffn_group = group_of(s, s0, 6 + p) if spiking else None

                def spikes_of(t):
                    f = ffn_group
                    if s0 >= B and t < STEPS - 1:
                        return
                    if t == 0 and s0 >= 10:
                        dve.wait_ge(counted, f - 1)
                    if t == STEPS - 1:
                        dve.wait_ge(spike_op_done, f * SPIKE_OPS + SPIKE_OPS)
                    dve.tensor_scalar(spikes[(s0 - 6 - p) // 2 % 2][:, t, :], mem[t][:], THRESHOLD, None, ALU.is_gt)\
                        .then_inc(spikes_ready, 1)

                def mem_free(t):
                    if s0 >= B and ffn_group > LATE and t < STEPS - 1:
                        dve.wait_ge(late_spikes_ready, late_spikes(ffn_group - 1, t + 1))

                def spike_op(n):
                    f = ffn_group
                    if n == 0:
                        dve.wait_ge(proj_done, f + 1)
                        if s0 >= 8:
                            dve.wait_ge(spike_op_done, f * SPIKE_OPS)
                        mem_free(0)
                        op = dve.tensor_copy(y_t[:], f_ps[0][:, 0:G * T])
                    else:
                        before, after = mem[(n - 1) // 2], mem[(n + 1) // 2]
                        dve.wait_ge(spike_op_done, f * SPIKE_OPS + n)
                        if n % 2:
                            op = dve.scalar_tensor_tensor(out=charge[:], in0=before[:], scalar=BETA, in1=y_t[:],
                                                          op0=ALU.mult, op1=ALU.add)
                        else:
                            mem_free(n // 2)
                            op = dve.scalar_tensor_tensor(out=mem[n // 2][:], in0=before[:], scalar=THRESHOLD,
                                                          in1=charge[:], op0=ALU.is_gt, op1=ALU.subtract, reverse1=True)
                    op.then_inc(spike_op_done, 1)
                    if n % 2:
                        spikes_of(n // 2)

                def evacuate_attn():
                    dve.wait_ge(pv_done, s)
                    if s0 >= 2:
                        dve.wait_ge(y_ready, s - 1)
                    dve.tensor_copy(attn_t[:], o_ps).then_inc(attn_t_ready, 1)

                def x2_of(b):
                    dve.wait_ge(y_ready, b + 1)
                    dve.wait_ge(bias_added, b + 1)
                    dve.scalar_tensor_tensor(out=seq(b), in0=y_ps, scalar=tanh_gates[:, 0:1], in1=seq(b),
                                             op0=ALU.mult, op1=ALU.add).then_inc(x2_ready, 1)

                def result(f):
                    dve.wait_ge(counted, f + 1)
                    xs = x_all[:, bass.ds(f * G, G), :]
                    dve.scalar_tensor_tensor(out=xs, in0=count_ps.rearrange("p (b d) -> p b d", b=G), scalar=spike_gain[:],
                                             in1=xs, op0=ALU.mult, op1=ALU.add).then_inc(result_ready, 1)

                first_op = 1 if on["spikes_a"] else 5
                if on["attend"]:
                    dve.wait_ge(exp_done, s * U)
                    if s0 >= 2:
                        dve.wait_ge(inv_ready, s - 1)
                    dve.reciprocal(inv_row[:], row_sum[:, 1 - p, :]).then_inc(inv_row_ready, 1)
                if s0 == B + 1:
                    spike_op(first_op)
                if on["turn"]:
                    x2_of(s - 2)
                if on["scores"]:
                    maxes(2, s, s0)
                if on["next_scores"]:
                    maxes(0, s + 1, s0 + 1)
                if on["turn"]:
                    if s0 >= 3:
                        dve.wait_ge(moments2_ready, s - 2)
                    dve.wait_ge(x2_ready, s - 1)
                    settle(dve)
                    dve.bn_stats(stats2[:], seq(s - 2)).then_inc(stats2_done, 1)
                if on["proj"] and s0 < B:
                    f = group_of(s, s0, 5)
                    dve.wait_ge(fc_done, f * 2 + 2)
                    if s0 >= 7:
                        dve.wait_ge(hidden_ready, f * 2)
                    dve.tensor_scalar(relu[:, 1, :], f_ps[1][:], 0.0, None, ALU.max).then_inc(relu_ready[1], 1)
                if on["spikes_a"]:
                    spike_op(0)
                if on["turn"]:
                    if s0 >= 3:
                        dve.wait_ge(centred_ready, s - 2)
                        dve.wait_ge(rstd2_ready, s - 2)
                    dve.wait_ge(stats2_done, s - 1)
                    settle(dve)
                    dve.bn_aggr(moments2[:], stats2[:]).then_inc(moments2_ready, 1)
                if spiking and s0 != B + 1:
                    spike_op(first_op)
                if on["finish"] and s0 < B + 2:
                    result(group_of(s, s0, 9))
                if spiking:
                    spike_op(first_op + 1)
                if s0 == 0:
                    q_last(NPG - 1)
                if on["attend"] and s0 < B:
                    evacuate_attn()
                if on["next_scores"]:
                    maxes(1, s + 1, s0 + 1)
                if s0 == B + 4:
                    result(NG - 2)
                if spiking:
                    spike_op(first_op + 2)
                    spike_op(first_op + 3)
                if on["spikes_b"]:
                    spikes_of(STEPS - 1)
                if s0 == B:
                    evacuate_attn()
                if s0 == B + 3:
                    result(NG - 3)
                if s0 == B + 6:
                    result(NG - 1)

            stage2(dve, slot)


_OUT = ((B, T, D), "float32")


def kernel(x, ctx_1024, g_xattn, g_ffn, L0_xattn_Wq, L0_xattn_bq, L0_xattn_Wk, L0_xattn_bk, L0_xattn_Wv,
           L0_xattn_bv, L0_xattn_Wc, L0_xattn_bc, L0_ffn_W_fc, L0_ffn_W_proj):
    import numpy as np
    import concourse.bacc as bacc
    from concourse.bass_utils import run_bass_kernel_spmd

    def t(a):
        return np.ascontiguousarray(np.asarray(a).T)

    def by_dim(a):
        return np.ascontiguousarray(np.asarray(a).reshape(H, ND, -1).transpose(1, 0, 2).reshape(D, -1))

    wc_rows = t(L0_xattn_Wc).reshape(2, TILES, 2 * ND, D).transpose(1, 0, 2, 3).reshape(D, D)
    w_proj = t(L0_ffn_W_proj).reshape(FF // 128, 128, D).transpose(1, 0, 2).reshape(128, FF)
    laid_out = dict(
        x=np.ascontiguousarray(x),
        ctxT=np.ascontiguousarray(np.asarray(ctx_1024).reshape(B * T, D).T),
        w_qkv=np.concatenate([t(by_dim(L0_xattn_Wk)), t(by_dim(L0_xattn_Wq)), t(L0_xattn_Wv),
                              by_dim(L0_xattn_bk), by_dim(L0_xattn_bq)], axis=1),
        vectors=np.concatenate([np.asarray(a) for a in (L0_xattn_bv, L0_xattn_bc, g_xattn, g_ffn)]),
        w_late=np.concatenate([wc_rows, t(L0_ffn_W_fc), w_proj], axis=1),
    )
    nc = bacc.Bacc("TRN2", target_bir_lowering=False, num_devices=1)
    arrays, args = {}, []
    for name, a in laid_out.items():
        arrays[f"in_{name}"] = a
        args.append(nc.dram_tensor(f"in_{name}", a.shape, mybir.dt.from_np(a.dtype), kind="ExternalInput").ap())
    args.append(nc.dram_tensor("out_0", _OUT[0], mybir.dt.from_np(np.dtype(_OUT[1])), kind="ExternalOutput").ap())
    gated_block_kernel(nc, *args)
    r = run_bass_kernel_spmd(nc, [arrays], core_ids=[0])
    return r.results[0]["out_0"]
```
